# Optimizing a Trainium2 kernel written in Bass

```python
import numpy as np
import jax
import jax.numpy as jnp

def _softmax(x, axis=-1):
    return jax.nn.softmax(x, axis=axis)

def _gelu(x):
    return jax.nn.gelu(x, approximate=True)

def _silu(x):
    return jax.nn.silu(x)

def _sigmoid(x):
    return jax.nn.sigmoid(x)

def _layernorm(x, axis=-1, eps=1e-05):
    m = jnp.mean(x, axis=axis, keepdims=True)
    v = jnp.var(x, axis=axis, keepdims=True)
    return (x - m) / jnp.sqrt(v + eps)

def _scatter_add(tgt, idx, src, axis=0):
    return tgt.at[idx].add(src)

def _segment_sum(src, seg, n):
    return jax.ops.segment_sum(src, seg, n)
kernel_name = 'mk_gnn_resnorm_d4_gnn_r8_2b8d7e'

def setup_inputs(seed: int=0):
    np.random.seed(seed)
    _w = jnp.asarray

    def _rec_inputs():
        import jax
        import jax.numpy as jnp
        _gk = jax.random.key(seed)
        x = -0.0005121 + 1.001 * jax.random.normal(jax.random.fold_in(_gk, 1), (6250, 64), jnp.float32)
        _s = jax.random.randint(jax.random.fold_in(_gk, 2), (100000,), 0, 6250, jnp.int32)
        _d = jax.random.randint(jax.random.fold_in(_gk, 3), (100000,), 0, 6250, jnp.int32)
        _loop = jnp.arange(6250, dtype=jnp.int32)
        src = jnp.concatenate([_s, _d, _loop])
        dst = jnp.concatenate([_d, _s, _loop])
        _o = jnp.argsort(dst, stable=True)
        src = src[_o]
        dst = dst[_o]
        edge_type_32 = jax.random.randint(jax.random.fold_in(_gk, 13), (206250,), 0, 32, jnp.int32)
        edge_weight1 = 0.000452788 + 0.999756 * jax.random.normal(jax.random.fold_in(_gk, 14), (206250, 1), jnp.float32)
        return (x, src, dst, edge_type_32, edge_weight1)
    x, src, dst, edge_type_32, edge_weight1 = _rec_inputs()

    def _L0_gnn_setup():
        import jax, jax.numpy as jnp
        import numpy as np
        N_NODES = 6250
        N_EDGES = 100000
        N_RELS = 32
        D_IN = 64
        D_OUT = 64
        key = jax.random.key(seed)
        k_feat, k_w, k_src, k_dst, k_et = jax.random.split(key, 5)
        feat = jax.random.normal(k_feat, (N_NODES, D_IN), dtype=jnp.float32)
        weight = jax.random.normal(k_w, (N_RELS, D_IN, D_OUT), dtype=jnp.float32) * 0.05
        src = jax.random.randint(k_src, (N_EDGES,), 0, N_NODES, dtype=jnp.int32)
        dst = jax.random.randint(k_dst, (N_EDGES,), 0, N_NODES, dtype=jnp.int32)
        etypes = jax.random.randint(k_et, (N_EDGES,), 0, N_RELS, dtype=jnp.int32)
        E_per_rel = jnp.bincount(etypes, length=N_RELS)
        return {'feat': feat, 'weight': weight, 'src': src, 'dst': dst, 'etypes': etypes, 'E_per_rel': E_per_rel}
    _L0_gnn_all = _L0_gnn_setup()
    _L0_gnn_in = {k: v for k, v in _L0_gnn_all.items() if k in ('weight', 'E_per_rel')}
    del _L0_gnn_all

    def _L1_gnn_setup():
        import jax, jax.numpy as jnp
        import numpy as np
        N_NODES = 12500

        def _gcn_norm(edge_index, num_nodes):
            loop = jnp.arange(num_nodes, dtype=edge_index.dtype)
            src = jnp.concatenate([edge_index[0], loop])
            dst = jnp.concatenate([edge_index[1], loop])
            deg = jax.ops.segment_sum(jnp.ones_like(src, dtype=jnp.float32), dst, num_segments=num_nodes)
            dinv = jnp.where(deg > 0, jax.lax.rsqrt(deg), 0.0)
            norm = dinv[src] * dinv[dst]
            return (src, dst, norm)
        key = jax.random.key(seed)
        ks = jax.random.split(key, 7)
        d = 64
        E = 125000
        x = jax.random.normal(ks[0], (N_NODES, d), dtype=jnp.float32)
        edge_index = jax.random.randint(ks[1], (2, E), 0, N_NODES, dtype=jnp.int64)
        s = 1.0 / np.sqrt(d)
        Ws = jax.random.normal(ks[2], (3, d, d), dtype=jnp.float32) * s
        bs = jax.random.normal(ks[3], (3, d), dtype=jnp.float32) * 0.02
        W_out = jax.random.normal(ks[4], (d, d), dtype=jnp.float32) * s
        b_out = jax.random.normal(ks[5], (d,), dtype=jnp.float32) * 0.02
        return {'x': x, 'edge_index': edge_index, 'Ws': Ws, 'bs': bs, 'W_out': W_out, 'b_out': b_out}
    _L1_gnn_all = _L1_gnn_setup()
    _L1_gnn_in = {k: v for k, v in _L1_gnn_all.items() if k in ('Ws', 'bs', 'W_out', 'b_out')}
    del _L1_gnn_all

    def _L2_gnn_setup():
        import jax, jax.numpy as jnp
        import numpy as np
        N = 12500
        E = 200000
        ND = 64
        ED = 1
        HD = 128
        key = jax.random.key(seed)
        ks = jax.random.split(key, 12)
        x = jax.random.normal(ks[0], (N, ND), dtype=jnp.float32)
        edge_index = jax.random.randint(ks[1], (2, E), 0, N, dtype=jnp.int32)
        edge_attr = jax.random.normal(ks[2], (E, ED), dtype=jnp.float32)
        s1 = 1.0 / np.sqrt(2 * ND + ED)
        W1 = jax.random.uniform(ks[3], (HD, 2 * ND + ED), minval=-s1, maxval=s1, dtype=jnp.float32)
        b1 = jax.random.uniform(ks[4], (HD,), minval=-s1, maxval=s1, dtype=jnp.float32)
        s2 = 1.0 / np.sqrt(HD)
        W2 = jax.random.uniform(ks[5], (ND, HD), minval=-s2, maxval=s2, dtype=jnp.float32)
        b2 = jax.random.uniform(ks[6], (ND,), minval=-s2, maxval=s2, dtype=jnp.float32)
        sg = 1.0 / np.sqrt(ND)
        W_ih = jax.random.uniform(ks[7], (3 * ND, ND), minval=-sg, maxval=sg, dtype=jnp.float32)
        b_ih = jax.random.uniform(ks[8], (3 * ND,), minval=-sg, maxval=sg, dtype=jnp.float32)
        W_hh = jax.random.uniform(ks[9], (3 * ND, ND), minval=-sg, maxval=sg, dtype=jnp.float32)
        b_hh = jax.random.uniform(ks[10], (3 * ND,), minval=-sg, maxval=sg, dtype=jnp.float32)
        return {'x': x, 'edge_index': edge_index, 'edge_attr': edge_attr, 'W1': W1, 'b1': b1, 'W2': W2, 'b2': b2, 'W_ih': W_ih, 'b_ih': b_ih, 'W_hh': W_hh, 'b_hh': b_hh}
    _L2_gnn_all = _L2_gnn_setup()
    _L2_gnn_in = {k: v for k, v in _L2_gnn_all.items() if k in ('W1', 'b1', 'W2', 'b2', 'W_ih', 'b_ih', 'W_hh', 'b_hh')}
    del _L2_gnn_all

    def _L3_gnn_setup():
        import jax, jax.numpy as jnp
        import numpy as np
        N = 6250
        E = 100000
        DIN = 64
        DOUT = 64
        key = jax.random.key(seed)
        k1, k2, k3 = jax.random.split(key, 3)
        x = jax.random.normal(k1, (N, DIN), dtype=jnp.float32)
        edge_index = jax.random.randint(k2, (2, E), 0, N, dtype=jnp.int32)
        limit = float(np.sqrt(6.0 / (DIN + DOUT)))
        weight = jax.random.uniform(k3, (DIN, DOUT), dtype=jnp.float32, minval=-limit, maxval=limit)
        bias = jnp.zeros((DOUT,), dtype=jnp.float32)
        return {'x': x, 'edge_index': edge_index, 'weight': weight, 'bias': bias}
    _L3_gnn_all = _L3_gnn_setup()
    _L3_gnn_in = {k: v for k, v in _L3_gnn_all.items() if k in ('weight', 'bias')}
    del _L3_gnn_all
    return {'x': x, 'src': src, 'dst': dst, 'edge_type_32': edge_type_32, 'edge_weight1': edge_weight1, 'L0_gnn_weight': _L0_gnn_in['weight'], 'L0_gnn_E_per_rel': _L0_gnn_in['E_per_rel'], 'L1_gnn_Ws': _L1_gnn_in['Ws'], 'L1_gnn_bs': _L1_gnn_in['bs'], 'L1_gnn_W_out': _L1_gnn_in['W_out'], 'L1_gnn_b_out': _L1_gnn_in['b_out'], 'L2_gnn_W1': _L2_gnn_in['W1'], 'L2_gnn_b1': _L2_gnn_in['b1'], 'L2_gnn_W2': _L2_gnn_in['W2'], 'L2_gnn_b2': _L2_gnn_in['b2'], 'L2_gnn_W_ih': _L2_gnn_in['W_ih'], 'L2_gnn_b_ih': _L2_gnn_in['b_ih'], 'L2_gnn_W_hh': _L2_gnn_in['W_hh'], 'L2_gnn_b_hh': _L2_gnn_in['b_hh'], 'L3_gnn_weight': _L3_gnn_in['weight'], 'L3_gnn_bias': _L3_gnn_in['bias']}

def reference(x, src, dst, edge_type_32, edge_weight1, L0_gnn_weight, L0_gnn_E_per_rel, L1_gnn_Ws, L1_gnn_bs, L1_gnn_W_out, L1_gnn_b_out, L2_gnn_W1, L2_gnn_b1, L2_gnn_W2, L2_gnn_b2, L2_gnn_W_ih, L2_gnn_b_ih, L2_gnn_W_hh, L2_gnn_b_hh, L3_gnn_weight, L3_gnn_bias):
    import jax
    import jax.numpy as jnp

    def _L0_gnn_ref(feat, weight, src, dst, etypes, E_per_rel):
        import jax, jax.numpy as jnp
        import numpy as np
        N_NODES = 6250
        N_EDGES = 100000
        N_RELS = 32
        D_IN = 64
        D_OUT = 64
        N = feat.shape[0]
        R, D_in, D_out = weight.shape
        gathered = feat[src]
        seg = dst.astype(jnp.int32) * R + etypes.astype(jnp.int32)
        per_node_rel = jax.ops.segment_sum(gathered, seg, num_segments=N * R)
        per_node_rel = per_node_rel.reshape(N, R, D_in)
        out = jnp.einsum('nri,rio->no', per_node_rel, weight)
        return out

    def _L1_gnn_ref(x, edge_index, Ws, bs, W_out, b_out):
        import jax, jax.numpy as jnp
        import numpy as np
        N_NODES = 12500

        def _gcn_norm(edge_index, num_nodes):
            loop = jnp.arange(num_nodes, dtype=edge_index.dtype)
            src = jnp.concatenate([edge_index[0], loop])
            dst = jnp.concatenate([edge_index[1], loop])
            deg = jax.ops.segment_sum(jnp.ones_like(src, dtype=jnp.float32), dst, num_segments=num_nodes)
            dinv = jnp.where(deg > 0, jax.lax.rsqrt(deg), 0.0)
            norm = dinv[src] * dinv[dst]
            return (src, dst, norm)
        num_nodes = x.shape[0]
        src, dst, norm = _gcn_norm(edge_index, num_nodes)
        for i in range(Ws.shape[0]):
            h = x @ Ws[i]
            msg = norm[:, None] * h[src]
            x = jax.ops.segment_sum(msg, dst, num_segments=num_nodes) + bs[i]
            x = jax.nn.relu(x)
        return x @ W_out + b_out

    def _L2_gnn_ref(x, edge_index, edge_attr, W1, b1, W2, b2, W_ih, b_ih, W_hh, b_hh):
        import jax, jax.numpy as jnp
        import numpy as np
        N = 12500
        E = 200000
        ND = 64
        ED = 1
        HD = 128
        src, dst = (edge_index[0], edge_index[1])
        m = jnp.concatenate([x[src], x[dst], edge_attr], axis=-1)
        m = jax.nn.relu(m @ W1.T + b1) @ W2.T + b2
        aggr = jnp.zeros_like(x).at[dst].add(m)
        gi = aggr @ W_ih.T + b_ih
        gh = x @ W_hh.T + b_hh
        i_r, i_z, i_n = jnp.split(gi, 3, axis=-1)
        h_r, h_z, h_n = jnp.split(gh, 3, axis=-1)
        r = jax.nn.sigmoid(i_r + h_r)
        z = jax.nn.sigmoid(i_z + h_z)
        n = jnp.tanh(i_n + r * h_n)
        return (1.0 - z) * n + z * x

    def _L3_gnn_ref(x, edge_index, weight, bias):
        import jax, jax.numpy as jnp
        import numpy as np
        N = 6250
        E = 100000
        DIN = 64
        DOUT = 64
        n = x.shape[0]
        row, col = (edge_index[0], edge_index[1])
        deg = jax.ops.segment_sum(jnp.ones_like(row, dtype=x.dtype), row, num_segments=n)
        dinv = jnp.where(deg > 0, jax.lax.rsqrt(deg), jnp.zeros_like(deg))
        xw = x @ weight
        msgs = (dinv[row] * dinv[col])[:, None] * xw[col]
        agg = jax.ops.segment_sum(msgs, row, num_segments=n)
        return agg + bias
    edge_index = jnp.stack([src, dst])
    x = _layernorm(x + _L0_gnn_ref(x, L0_gnn_weight, src, dst, edge_type_32, L0_gnn_E_per_rel), axis=-1)
    x = _layernorm(x + _L1_gnn_ref(x, edge_index, L1_gnn_Ws, L1_gnn_bs, L1_gnn_W_out, L1_gnn_b_out), axis=-1)
    x = _layernorm(x + _L2_gnn_ref(x, edge_index, edge_weight1, L2_gnn_W1, L2_gnn_b1, L2_gnn_W2, L2_gnn_b2, L2_gnn_W_ih, L2_gnn_b_ih, L2_gnn_W_hh, L2_gnn_b_hh), axis=-1)
    x = _layernorm(x + _L3_gnn_ref(x, edge_index, L3_gnn_weight, L3_gnn_bias), axis=-1)
    return x

_drawn_inputs = setup_inputs


def setup_inputs(seed=0):
    import zlib

    import numpy as np

    out = dict(_drawn_inputs(seed))
    spreads = {'L3_gnn_bias': (0.0, 0.1)}
    factors = {'edge_weight1': 4.856, 'L1_gnn_bs': 4.108, 'L2_gnn_b_ih': 3.473, 'L2_gnn_b_hh': 5.232}
    for name, (base, spread) in spreads.items():
        noise = np.random.default_rng([zlib.crc32(name.encode()), seed]).standard_normal(out[name].shape)
        drawn = base * np.exp(spread * noise) if base else spread * noise
        out[name] = jnp.asarray(drawn.astype(out[name].dtype))
    for name, factor in factors.items():
        out[name] = (out[name] * factor).astype(out[name].dtype)
    return out
```

```python
import concourse.bass as bass
import numpy as np
from concourse import mybir
from concourse.alu_op_type import AluOpType as ALU
from contextlib import ExitStack

F32 = mybir.dt.float32
I32 = mybir.dt.int32
ACT = mybir.ActivationFunctionType
AX = mybir.AxisListType
P = 128
N = 6250
E = 206250
D = 64
HID = 128
R = 32
NB = (N + P - 1) // P
NP = NB * P
ET = (E + P - 1) // P
HALF = 13
RING = 2 * HALF
ITER = ET // RING
assert ITER * RING == ET
EPS = 1e-5
BANK = 512


class Mem:
    pass


def alloc(nc, ctx):
    m = Mem()

    def sb(name, shape, dt=F32):
        return ctx.enter_context(nc.sbuf_tensor(name, shape, dt))

    m.src = sb("src", [P, ET], I32)
    m.dst = sb("dst", [P, ET], I32)
    m.rel = sb("rel", [P, ET], I32)
    m.src_rel = sb("src_rel", [P, ET], I32)
    m.attr = sb("attr", [P, ET])
    m.local = sb("local", [P, ET])
    m.stage = sb("stage", [P, RING], I32)
    m.feat = sb("feat", [P, RING, HID])
    m.onehot = sb("onehot", [P, RING, P])
    m.acc = sb("acc", [P, NP + P])
    m.xT = sb("xT", [D, NP])
    m.x = sb("x", [P, NB, D])
    m.cur = sb("cur", [P, NB, D])
    m.h = sb("h", [P, NB, D])
    m.rows = sb("rows", [P, NB, HID])
    m.tmp = sb("tmp", [P, NB, D])
    m.deg = sb("deg", [P, NB])
    m.dinv1 = sb("dinv1", [P, NB])
    m.dinv3 = sb("dinv3", [P, NB])
    m.st = [sb(f"st{i}", [P, NB]) for i in range(3)]
    m.ident = sb("ident", [P, P])
    m.iota = sb("iota", [P, P])
    m.iota_p = sb("iota_p", [P, 1])
    m.ones = sb("ones", [1, P])
    m.w0 = sb("w0", [D, R * D])
    m.w1 = sb("w1", [D, 3, D])
    m.wout = sb("wout", [D, D])
    m.b1 = sb("b1", [P, 3, D])
    m.bout = sb("bout", [P, D])
    m.wa = sb("wa", [D, HID])
    m.wb = sb("wb", [D, HID])
    m.wc = sb("wc", [P, HID])
    m.bh = sb("bh", [P, HID])
    m.w2 = sb("w2", [HID, D])
    m.b2 = sb("b2", [P, D])
    m.wih = sb("wih", [D, 3 * D])
    m.whh = sb("whh", [D, 3 * D])
    m.bih = sb("bih", [P, 3 * D])
    m.bhh = sb("bhh", [P, 3 * D])
    m.w3 = sb("w3", [D, D])
    m.b3 = sb("b3", [P, D])
    m.ps = ctx.enter_context(nc.psum_tensor("ps", [P, 8, BANK], F32))

    def sem(name):
        return ctx.enter_context(nc.semaphore(name))

    m.landed = [sem(f"landed{u}") for u in range(RING)]
    m.staged = sem("staged")
    m.compared, m.summed, m.added = sem("compared"), sem("summed"), sem("added")
    m.passes = 0
    m.multiplied = sem("multiplied")
    m.copied = [sem("dve_copied"), sem("act_copied")]
    m.groups, m.copies = 0, [0, 0]
    return m


def load(nc, m, a):
    with nc.semaphore("loaded") as loaded, nc.semaphore("iotas") as iotas, nc.semaphore("ready") as ready, \
            nc.semaphore("based") as based, nc.semaphore("ident_zero") as ident_zero, nc.Block() as block:
        row_bias = [(m.bout, "bout"), (m.bh, "bh"), (m.b2, "b2"), (m.bih, "bih"), (m.bhh, "bhh"), (m.b3, "b3"),
                    (m.wc, "wc")]
        plain = [(m.src, "src"), (m.dst, "dst"), (m.rel, "rel"), (m.attr, "attr"), (m.xT, "xT"), (m.w0, "w0"),
                 (m.w1, "w1"), (m.wout, "wout"), (m.wa, "wa"), (m.wb, "wb"), (m.w2, "w2"), (m.wih, "wih"),
                 (m.whh, "whh"), (m.w3, "w3")]
        total = 16 * (len(row_bias) + len(plain) + 2)

        @block.sync
        def _(sp):
            for t, name in plain:
                sp.dma_start(t[:], a[name]).then_inc(loaded, 16)
            sp.dma_start(m.x[:], a["x"].rearrange("(b p) d -> p b d", p=P)).then_inc(loaded, 16)
            for t, name in row_bias:
                sp.dma_start(t[:], a[name].partition_broadcast(P)).then_inc(loaded, 16)
            sp.dma_start(m.b1[:], a["b1"].partition_broadcast(P)).then_inc(loaded, 16)

        @block.gpsimd
        def _(pool):
            pool.iota(m.iota[:], [[1, P]], base=0, channel_multiplier=0,
                      allow_small_or_imprecise_dtypes=True).then_inc(iotas, 1)
            pool.iota(m.iota_p[:], [[1, 1]], base=0, channel_multiplier=1,
                      allow_small_or_imprecise_dtypes=True).then_inc(iotas, 1)
            pool.memset(m.ident[:], 0.0).then_inc(ident_zero, 1)
            pool.wait_ge(ident_zero, 1)
            pool.affine_select(out=m.ident[:], in_=m.ident[:], compare_op=ALU.not_equal, fill=1.0, base=0,
                               pattern=[[-1, P]], channel_multiplier=1).then_inc(iotas, 1)

        @block.tensor
        def _(pe):
            pe.wait_ge(ready, 3)
            for c in range(4):
                w = ET // 4
                nc.tensor.matmul(m.ps[:, c, 0:w], m.ones[:], m.tmp[0:1, :, :].rearrange("p b d -> p (b d)")[:, c * w:(c + 1) * w],
                                 start=True, stop=True).then_inc(based, 1)

        @block.vector
        def _(dve):
            dve.memset(m.ones[:], 1.0).then_inc(ready, 1)
            dve.memset(m.feat[:], 1.0)
            dve.wait_ge(loaded, total)
            dve.tensor_copy(m.tmp[0:1, :, :].rearrange("p b d -> p (b d)")[:, 0:ET], m.dst[0:1, :]).then_inc(ready, 1)
            dve.scalar_tensor_tensor(m.src_rel[:], m.src[:], float(R), m.rel[:], op0=ALU.mult, op1=ALU.add)
            dve.tensor_copy(m.local[:], m.dst[:]).then_inc(ready, 1)
            dve.wait_ge(ready, 3)
            dve.wait_ge(based, 4)
            w = ET // 4
            for c in range(4):
                dve.tensor_tensor(m.local[:, c * w:(c + 1) * w], m.local[:, c * w:(c + 1) * w], m.ps[:, c, 0:w],
                                  ALU.subtract)

        @block.scalar
        def _(act):
            act.wait_ge(iotas, 3)
            act.wait_ge(loaded, total)


def relation_table(nc, m, table):
    y = m.rows[:, 0:2 * R * D // HID, :].rearrange("p b d -> p (b d)").rearrange("p (k c) -> p k c", k=2)
    with nc.semaphore("rel_multiplied") as multiplied, \
            nc.semaphore("rel_act_copied") as act_copied, nc.semaphore("rel_dve_copied") as dve_copied, \
            nc.semaphore("stored0") as stored0, nc.semaphore("stored1") as stored1, nc.Block() as block:
        stored = [stored0, stored1]
        t = table.rearrange("(n r) d -> n (r d)", r=R)
        half = R * D // 2

        @block.tensor
        def _(pe):
            for b in range(NB):
                if b >= 2:
                    pe.wait_ge(act_copied, b - 1)
                    pe.wait_ge(dve_copied, b - 1)
                for q in range(4):
                    k = nc.tensor.matmul(m.ps[:, 4 * (b % 2) + q, :], m.xT[:, b * P:(b + 1) * P],
                                         m.w0[:, q * BANK:(q + 1) * BANK], start=True, stop=True)
                k.then_inc(multiplied, 1)

        def copy(e, b, copied, lo):
            e.wait_ge(multiplied, b + 1)
            if b >= 2:
                e.wait_ge(stored[b % 2], 16 * (b // 2))
            o = y[:, b % 2, lo * half:(lo + 1) * half]
            i = m.ps[:, 4 * (b % 2) + 2 * lo:4 * (b % 2) + 2 * lo + 2, :].rearrange("p q c -> p (q c)")
            (e.copy(o, i) if lo else e.tensor_copy(o, i)).then_inc(copied, 1)

        @block.vector
        def _(dve):
            for b in range(NB):
                copy(dve, b, dve_copied, 0)

        @block.scalar
        def _(act):
            for b in range(NB):
                copy(act, b, act_copied, 1)

        @block.sync
        def _(sp):
            for b in range(NB):
                sp.wait_ge(act_copied, b + 1)
                sp.wait_ge(dve_copied, b + 1)
                sp.dma_start(t[b * P:(b + 1) * P, :], y[:, b % 2, :]).then_inc(stored[b % 2], 16)
            for i in range(2):
                sp.wait_ge(stored[i], 16 * ((NB + 1 - i) // 2))


def edge_sum(nc, m, table, index, width, rows):
    with ExitStack() as ctx:
        cleared = ctx.enter_context(nc.semaphore("cleared"))
        landed, staged, compared, summed, added = m.landed, m.staged, m.compared, m.summed, m.added
        tiles0, iters0 = m.passes * ET, m.passes * ITER
        m.passes += 1
        block = ctx.enter_context(nc.Block())

        @block.scalar
        def _(act):
            def stage(i, first):
                for h in range(2):
                    if not first:
                        act.wait_ge(summed, tiles0 + RING * (i - 1) + HALF * (h + 1))
                    act.copy(m.stage[:, h * HALF:(h + 1) * HALF],
                             index[:, bass.ds(i * RING + h * HALF, HALF)]).then_inc(staged, 1)
            stage(0, True)
            with act.Fori(1, ITER) as i:
                stage(i, False)

        @block.gpsimd
        def _(pool):
            def gather(i):
                for u in range(RING):
                    if u % HALF == 0:
                        pool.wait_ge(staged, 2 * iters0 + 2 * i + u // HALF + 1)
                        pool.nop(nofuse=True)
                    pool.indirect_dma_start(m.feat[:, u, 0:width], None, table,
                                            bass.IndirectOffsetOnAxis(ap=m.stage[:, u:u + 1], axis=0)
                                            ).then_inc(landed[u], 16)
            gather(0)
            with pool.Fori(1, ITER) as i:
                gather(i)

        @block.tensor
        def _(pe):
            def tiles(i, first):
                for u in range(RING):
                    pe.wait_ge(landed[u], 16 * iters0 + 16 * i + 16)
                    pe.wait_ge(compared, tiles0 + RING * i + u + 1)
                    if not (first and u < 2):
                        pe.wait_ge(added, tiles0 + RING * i + u - 1)
                    nc.tensor.matmul(m.ps[0:rows, u % 2, 0:P], m.feat[:, u, 0:rows], m.onehot[:, u, :],
                                     start=True, stop=True).then_inc(summed, 1)
            tiles(0, True)
            with pe.Fori(1, ITER) as i:
                tiles(i, False)

        @block.vector
        def _(dve):
            def compare(i, u):
                dve.tensor_scalar(m.onehot[:, u, :], m.iota[:], m.local[:, bass.ds(i * RING + u, 1)], None,
                                  ALU.is_equal).then_inc(compared, 1)

            def add(i, u, first):
                base = dve.value_load(m.dst[0:1, bass.ds(i * RING + u, 1)], min_val=0, max_val=N - 1)
                dve.wait_ge(summed, tiles0 + RING * i + u + 1)
                if not (first and u == 0):
                    dve.wait_ge(added, tiles0 + RING * i + u)
                window = m.acc[0:rows, bass.ds(base, P)]
                dve.tensor_tensor(window, window, m.ps[0:rows, u % 2, 0:P], ALU.add).then_inc(added, 1)

            dve.memset(m.acc[0:rows, :], 0.0).then_inc(cleared, 1)
            for u in range(RING):
                compare(0, u)
            dve.wait_ge(cleared, 1)

            def tiles(i, first):
                for u in range(RING):
                    add(i, u, first)
                    compare(i + 1, u)
            tiles(0, True)
            with dve.Fori(1, ITER - 1) as i:
                tiles(i, False)
            for u in range(RING):
                add(ITER - 1, u, False)


def edge_mlp_sum(nc, m, table, q):
    with ExitStack() as ctx:
        sem = lambda name: ctx.enter_context(nc.semaphore(name))
        landed, staged, compared, summed, added = m.landed, m.staged, m.compared, m.summed, m.added
        tiles0, iters0 = m.passes * ET, m.passes * ITER
        m.passes += 1
        fetched = [sem(f"fetched{u}") for u in range(HALF)]
        names = ("cleared", "spread", "turned", "hidden", "biased", "activated")
        cleared, spread, turned, hidden, biased, activated = map(sem, names)
        flat = m.h[:].rearrange("p b d -> p (b d)").rearrange("p (k c) -> p k c", c=HID) if NB % 2 == 0 else \
            m.h[:, 0:NB - 1, :].rearrange("p (k two) d -> p k (two d)", two=2)
        other = m.tmp[:, 0:NB - 1, :].rearrange("p (k two) d -> p k (two d)", two=2)
        window_q = flat[:, 0:HALF, :]
        turned_hot = other[:, 0:2, :]
        act_in = other[:, 2:4, :]
        act_out = other[:, 4:6, :]
        block = ctx.enter_context(nc.Block())

        @block.scalar
        def _(act):
            def relu(i, u, first):
                act.wait_ge(hidden, RING * i + u + 1)
                if not (first and u < 2):
                    act.wait_ge(summed, tiles0 + RING * i + u - 1)
                act.activation(act_out[:, u % 2, :], m.ps[:, 4 + u % 2, 0:HID], ACT.Relu).then_inc(activated, 1)

            for h in range(2):
                act.copy(m.stage[:, h * HALF:(h + 1) * HALF],
                         m.src[:, h * HALF:(h + 1) * HALF]).then_inc(staged, 1)

            def body(i, first, last):
                for u in range(RING):
                    relu(i, u, first)
                    if u % HALF == HALF - 1 and not last:
                        h = u // HALF
                        act.copy(m.stage[:, h * HALF:(h + 1) * HALF],
                                 m.src[:, bass.ds((i + 1) * RING + h * HALF, HALF)]).then_inc(staged, 1)
            body(0, True, False)
            with act.Fori(1, ITER - 1) as i:
                body(i, False, False)
            body(ITER - 1, False, True)

        @block.gpsimd
        def _(pool):
            def gather(i):
                for u in range(RING):
                    if u % HALF == 0:
                        pool.wait_ge(staged, 2 * iters0 + 2 * i + u // HALF + 1)
                        pool.nop(nofuse=True)
                    pool.indirect_dma_start(m.feat[:, u, :], None, table,
                                            bass.IndirectOffsetOnAxis(ap=m.stage[:, u:u + 1], axis=0)
                                            ).then_inc(landed[u], 16)
            gather(0)
            with pool.Fori(1, ITER) as i:
                gather(i)

        @block.sync
        def _(sp):
            def fetch(i, first):
                for u in range(RING):
                    base = sp.value_load(m.dst[0:1, bass.ds(i * RING + u, 1)], min_val=0, max_val=N - 1)
                    if not (first and u < HALF):
                        sp.wait_ge(hidden, RING * i + u + 1 - HALF)
                    sp.dma_start(window_q[:, u % HALF, :], q[bass.ds(base, P), :]).then_inc(fetched[u % HALF], 16)
            fetch(0, True)
            with sp.Fori(1, ITER) as i:
                fetch(i, False)

        @block.tensor
        def _(pe):
            def tiles(i, first):
                for u in range(RING):
                    pe.wait_ge(compared, tiles0 + RING * i + u + 1)
                    if not (first and u < 2):
                        pe.wait_ge(turned, RING * i + u - 1)
                    nc.tensor.transpose(m.ps[:, 2 + u % 2, 0:P], m.onehot[:, u, :], m.ident[:]).then_inc(spread, 1)
                    if not (first and u < 2):
                        pe.wait_ge(activated, RING * i + u - 1)
                    pe.wait_ge(biased, RING * i + u + 1)
                    nc.tensor.matmul(m.ps[:, 4 + u % 2, 0:HID], m.ident[:], act_in[:, u % 2, :], start=True, stop=False)
                    pe.wait_ge(turned, RING * i + u + 1)
                    pe.wait_ge(fetched[u % HALF], 32 * i + 16 * (u // HALF) + 16)
                    nc.tensor.matmul(m.ps[:, 4 + u % 2, 0:HID], turned_hot[:, u % 2, :], window_q[:, u % HALF, :],
                                     start=False, stop=True).then_inc(hidden, 1)
                    if not (first and u < 2):
                        pe.wait_ge(added, tiles0 + RING * i + u - 1)
                    pe.wait_ge(activated, RING * i + u + 1)
                    nc.tensor.matmul(m.ps[:, u % 2, 0:P], act_out[:, u % 2, :], m.onehot[:, u, :], start=True,
                                     stop=True).then_inc(summed, 1)
            tiles(0, True)
            with pe.Fori(1, ITER) as i:
                tiles(i, False)

        @block.vector
        def _(dve):
            def compare(i, u):
                dve.tensor_scalar(m.onehot[:, u, :], m.iota[:], m.local[:, bass.ds(i * RING + u, 1)], None,
                                  ALU.is_equal).then_inc(compared, 1)

            def front(i, u, first):
                dve.wait_ge(landed[u], 16 * iters0 + 16 * i + 16)
                if not (first and u < 2):
                    dve.wait_ge(hidden, RING * i + u - 1)
                dve.scalar_tensor_tensor(act_in[:, u % 2, :], m.wc[:], m.attr[:, bass.ds(i * RING + u, 1)],
                                         m.feat[:, u, :], op0=ALU.mult, op1=ALU.add).then_inc(biased, 1)
                dve.wait_ge(spread, RING * i + u + 1)
                dve.tensor_copy(turned_hot[:, u % 2, :], m.ps[:, 2 + u % 2, 0:P]).then_inc(turned, 1)

            def add(i, u, first):
                base = dve.value_load(m.dst[0:1, bass.ds(i * RING + u, 1)], min_val=0, max_val=N - 1)
                dve.wait_ge(summed, tiles0 + RING * i + u + 1)
                if not (first and u == 0):
                    dve.wait_ge(added, tiles0 + RING * i + u)
                window = m.acc[:, bass.ds(base, P)]
                dve.tensor_tensor(window, window, m.ps[:, u % 2, 0:P], ALU.add).then_inc(added, 1)

            dve.memset(m.acc[:], 0.0).then_inc(cleared, 1)
            for u in range(RING):
                compare(0, u)
            dve.wait_ge(cleared, 1)

            def tiles(i, first, last):
                for u in range(RING):
                    front(i, u, first)
                    add(i, u, first)
                    if not last:
                        compare(i + 1, u)
            tiles(0, True, False)
            with dve.Fori(1, ITER - 1) as i:
                tiles(i, False, False)
            tiles(ITER - 1, False, True)


def products(nc, m, name, width, per_bank, operands, dest):
    groups = [range(g, min(g + per_bank, NB)) for g in range(0, NB, per_bank)]
    multiplied, copied = m.multiplied, m.copied
    groups0, copies0 = m.groups, list(m.copies)
    m.groups += len(groups)
    m.copies = [copies0[k] + (len(groups) + 1 - k) // 2 for k in range(2)]
    with nc.Block() as block:
        @block.tensor
        def _(pe):
            for g, blocks in enumerate(groups):
                if g >= 8:
                    pe.wait_ge(copied[g % 2], copies0[g % 2] + (g - 8) // 2 + 1)
                for j, b in enumerate(blocks):
                    pairs = operands(b)
                    for k, (w, x) in enumerate(pairs):
                        last = nc.tensor.matmul(m.ps[0:w.shape[1], g % 8, j * width:(j + 1) * width], w, x,
                                                start=k == 0, stop=k == len(pairs) - 1)
                last.then_inc(multiplied, 1)

        def copy(e, g, put):
            blocks = groups[g]
            e.wait_ge(multiplied, groups0 + g + 1)
            rows = operands(0)[0][0].shape[1]
            put(dest(blocks[0], len(blocks)), m.ps[0:rows, g % 8, 0:len(blocks) * width]).then_inc(copied[g % 2], 1)

        @block.vector
        def _(dve):
            for g in range(0, len(groups), 2):
                copy(dve, g, dve.tensor_copy)

        @block.scalar
        def _(act):
            for g in range(1, len(groups), 2):
                copy(act, g, act.copy)


def transpose_rows(nc, m, rows, out=None):
    out = m.xT if out is None else out
    products(nc, m, "turn", P, 4, lambda b: [(rows[:, b, :], m.ident[:])],
             lambda b, n: out[:, b * P:(b + n) * P])


def project(nc, m, w, out, width):
    per = BANK // width
    products(nc, m, "project", width, per, lambda b: [(m.xT[:, b * P:(b + 1) * P], w)],
             lambda b, n: out[:, b:b + n, 0:width].rearrange("p b d -> p (b d)") if out.shape[2] == width
             else out[:, b:b + n, 0:width])


def sums_to_rows(nc, m, k, w, out, width):
    products(nc, m, "sums", width, BANK // width, lambda b: [(m.acc[0:k, b * P:(b + 1) * P], w)],
             lambda b, n: out[:, b:b + n, 0:width])


def per_node(t):
    return t[:, :].unsqueeze(2).broadcast_to([P, NB, D])


def per_feature(t, width=D):
    return t.unsqueeze(1).broadcast_to([P, NB, width])


def layer_norm(nc, m, update, out_dram=None):
    total, mean, rstd = m.st
    with nc.semaphore("step") as step, nc.semaphore("stored") as stored, nc.Block() as block:
        @block.vector
        def _(dve):
            dve.tensor_tensor(m.x[:], m.x[:], update, ALU.add).then_inc(step, 1)
            dve.wait_ge(step, 1)
            dve.tensor_reduce(total[:], m.x[:], axis=AX.X, op=ALU.add).then_inc(step, 1)
            dve.wait_ge(step, 2)
            dve.tensor_scalar(mean[:], total[:], 1.0 / D, None, ALU.mult).then_inc(step, 1)
            dve.wait_ge(step, 3)
            dve.tensor_tensor(m.x[:], m.x[:], per_node(mean), ALU.subtract).then_inc(step, 1)
            dve.wait_ge(step, 5)
            dve.tensor_reduce(total[:], m.tmp[:], axis=AX.X, op=ALU.add).then_inc(step, 1)
            dve.wait_ge(step, 6)
            dve.tensor_scalar(total[:], total[:], 1.0 / D, EPS, ALU.mult, ALU.add).then_inc(step, 1)
            dve.wait_ge(step, 8)
            dve.reciprocal(rstd[:], mean[:]).then_inc(step, 1)
            dve.wait_ge(step, 9)
            dve.tensor_tensor(m.x[:], m.x[:], per_node(rstd), ALU.mult).then_inc(step, 1)

        @block.scalar
        def _(act):
            act.wait_ge(step, 4)
            act.activation(m.tmp[:], m.x[:], ACT.Square).then_inc(step, 1)
            act.wait_ge(step, 7)
            act.activation(mean[:], total[:], ACT.Sqrt).then_inc(step, 1)

        if out_dram is not None:
            @block.sync
            def _(sp):
                sp.wait_ge(step, 10)
                full = N // P
                sp.dma_start(out_dram[0:full * P, :].rearrange("(b p) d -> p b d", p=P),
                             m.x[:, 0:full, :]).then_inc(stored, 16)
                sp.dma_start(out_dram[full * P:N, :], m.x[0:N - full * P, full, :]).then_inc(stored, 16)
                sp.wait_ge(stored, 32)


def degrees(nc, m):
    with nc.semaphore("step") as step, nc.Block() as block:
        @block.vector
        def _(dve):
            dve.tensor_copy(m.deg[:], m.rows[:, :, D]).then_inc(step, 1)
            dve.wait_ge(step, 1)
            dve.tensor_scalar(m.st[0][:], m.deg[:], 1.0, None, ALU.add).then_inc(step, 1)
            dve.tensor_scalar(m.st[1][:], m.deg[:], 1.0, None, ALU.max).then_inc(step, 1)
            dve.wait_ge(step, 5)
            dve.reciprocal(m.dinv1[:], m.st[2][:]).then_inc(step, 1)
            dve.reciprocal(m.st[0][:], m.dinv3[:]).then_inc(step, 1)
            dve.wait_ge(step, 7)
            dve.scalar_tensor_tensor(m.dinv3[:], m.deg[:], 0.0, m.st[0][:], op0=ALU.is_gt, op1=ALU.mult)

        @block.scalar
        def _(act):
            act.wait_ge(step, 3)
            act.activation(m.st[2][:], m.st[0][:], ACT.Sqrt).then_inc(step, 1)
            act.activation(m.dinv3[:], m.st[1][:], ACT.Sqrt).then_inc(step, 1)


def scale_and_store(nc, m, rows, scale, table, bias=None, width=D):
    with nc.semaphore("scaled") as scaled, nc.semaphore("stored") as stored, nc.Block() as block:
        @block.vector
        def _(dve):
            if scale is not None:
                dve.tensor_tensor(rows, rows, per_node(scale), ALU.mult).then_inc(scaled, 1)
            if bias is not None:
                dve.tensor_tensor(rows, rows, per_feature(bias, width), ALU.add).then_inc(scaled, 1)

        @block.sync
        def _(sp):
            if scale is not None or bias is not None:
                sp.wait_ge(scaled, 1)
            sp.dma_start(table[0:NP, :].rearrange("(b p) d -> p b d", p=P), rows).then_inc(stored, 16)
            sp.wait_ge(stored, 16)


def gcn_finish(nc, m, bias):
    r = m.rows[:, :, 0:D]
    with nc.semaphore("step") as step, nc.Block() as block:
        @block.vector
        def _(dve):
            dve.tensor_tensor(m.cur[:], r, m.h[:], ALU.add).then_inc(step, 1)
            dve.wait_ge(step, 1)
            dve.tensor_tensor(m.cur[:], m.cur[:], per_node(m.dinv1), ALU.mult).then_inc(step, 1)
            dve.wait_ge(step, 2)
            dve.tensor_tensor(m.cur[:], m.cur[:], per_feature(bias), ALU.add).then_inc(step, 1)
            dve.wait_ge(step, 3)
            dve.tensor_scalar(m.cur[:], m.cur[:], 0.0, None, ALU.max)


def add_bias(nc, m, rows, bias, scale=None, by_degree=False):
    with nc.semaphore("step") as step, nc.Block() as block:
        @block.vector
        def _(dve):
            if scale is not None:
                dve.tensor_tensor(rows, rows, per_node(scale), ALU.mult).then_inc(step, 1)
                dve.wait_ge(step, 1)
            if by_degree:
                dve.tensor_tensor(m.tmp[:], per_feature(bias), per_node(m.deg), ALU.mult).then_inc(step, 1)
                dve.wait_ge(step, 1)
                dve.tensor_tensor(rows, rows, m.tmp[:], ALU.add)
            else:
                dve.tensor_tensor(rows, rows, per_feature(bias), ALU.add)


def gru(nc, m, aggrT):
    r, z, n = m.h, m.tmp, m.rows
    rz = lambda lo: (m.bih[:, lo:lo + D], m.bhh[:, lo:lo + D])
    for lo, out in ((0, r), (D, z)):
        products(nc, m, "gate", D, 8, lambda b: [(aggrT[:, b * P:(b + 1) * P], m.wih[:, lo:lo + D]),
                                                (m.xT[:, b * P:(b + 1) * P], m.whh[:, lo:lo + D])],
                 lambda b, k: out[:, b:b + k, :].rearrange("p b d -> p (b d)"))
    products(nc, m, "new_in", D, 8, lambda b: [(aggrT[:, b * P:(b + 1) * P], m.wih[:, 2 * D:3 * D])],
             lambda b, k: n[:, b:b + k, 0:D])
    products(nc, m, "new_state", D, 8, lambda b: [(m.xT[:, b * P:(b + 1) * P], m.whh[:, 2 * D:3 * D])],
             lambda b, k: n[:, b:b + k, D:2 * D])
    i_n, h_n = n[:, :, 0:D], n[:, :, D:2 * D]
    with nc.semaphore("step") as step, nc.Block() as block:
        @block.vector
        def _(dve):
            at = 0
            for lo, g in ((0, r), (D, z)):
                for b in rz(lo):
                    if at:
                        dve.wait_ge(step, at)
                    dve.tensor_tensor(g[:], g[:], per_feature(b), ALU.add).then_inc(step, 1)
                    at += 1
            for part, b in ((i_n, m.bih), (h_n, m.bhh)):
                dve.tensor_tensor(part, part, per_feature(b[:, 2 * D:3 * D]), ALU.add).then_inc(step, 1)
            dve.wait_ge(step, 8)
            dve.tensor_tensor(h_n, h_n, r[:], ALU.mult).then_inc(step, 1)
            dve.wait_ge(step, 9)
            dve.tensor_tensor(h_n, h_n, i_n, ALU.add).then_inc(step, 1)
            dve.wait_ge(step, 11)
            dve.tensor_tensor(m.cur[:], m.x[:], h_n, ALU.subtract).then_inc(step, 1)
            dve.wait_ge(step, 12)
            dve.tensor_tensor(m.cur[:], m.cur[:], z[:], ALU.mult).then_inc(step, 1)
            dve.wait_ge(step, 13)
            dve.tensor_tensor(m.cur[:], m.cur[:], h_n, ALU.add)

        @block.scalar
        def _(act):
            act.wait_ge(step, 6)
            act.activation(r[:], r[:], ACT.Sigmoid).then_inc(step, 1)
            act.activation(z[:], z[:], ACT.Sigmoid).then_inc(step, 1)
            act.wait_ge(step, 10)
            act.activation(h_n, h_n, ACT.Tanh).then_inc(step, 1)


def build(nc, a, out):
    rel_table = nc.dram_tensor("rel_table", (NP * R, D), F32).ap()
    h_table = nc.dram_tensor("h_table", (NP, D), F32).ap()
    p_table = nc.dram_tensor("p_table", (NP, HID), F32).ap()
    q_table = nc.dram_tensor("q_table", (NP + P, HID), F32).ap()
    with ExitStack() as ctx:
        m = alloc(nc, ctx)
        load(nc, m, a)
        relation_table(nc, m, rel_table)
        edge_sum(nc, m, rel_table, m.src_rel, D, D + 1)
        sums_to_rows(nc, m, D + 1, m.ident[0:D + 1, 0:D + 1], m.rows, D + 1)
        degrees(nc, m)
        layer_norm(nc, m, m.rows[:, :, 0:D])
        for i in range(3):
            transpose_rows(nc, m, m.cur if i else m.x)
            project(nc, m, m.w1[:, i, :], m.h, D)
            scale_and_store(nc, m, m.h[:], m.dinv1, h_table)
            edge_sum(nc, m, h_table, m.src, D, D)
            sums_to_rows(nc, m, D, m.ident[0:D, 0:D], m.rows, D)
            gcn_finish(nc, m, m.b1[:, i, :])
        transpose_rows(nc, m, m.cur)
        project(nc, m, m.wout[:], m.h, D)
        add_bias(nc, m, m.h[:], m.bout[:])
        layer_norm(nc, m, m.h[:])
        transpose_rows(nc, m, m.x)
        project(nc, m, m.wa[:], m.rows, HID)
        scale_and_store(nc, m, m.rows[:], None, p_table)
        project(nc, m, m.wb[:], m.rows, HID)
        scale_and_store(nc, m, m.rows[:], None, q_table, bias=m.bh[:], width=HID)
        with nc.semaphore("padded") as padded, nc.Block() as block:
            @block.sync
            def _(sp):
                sp.dma_start(q_table[NP:NP + P, :], m.ident[:]).then_inc(padded, 16)
                sp.wait_ge(padded, 16)
        edge_mlp_sum(nc, m, p_table, q_table)
        sums_to_rows(nc, m, HID, m.w2[:], m.cur, D)
        add_bias(nc, m, m.cur[:], m.b2[:], by_degree=True)
        transpose_rows(nc, m, m.cur, m.acc[0:D, 0:NP])
        gru(nc, m, m.acc[0:D, 0:NP])
        layer_norm(nc, m, m.cur[:])
        transpose_rows(nc, m, m.x)
        project(nc, m, m.w3[:], m.h, D)
        scale_and_store(nc, m, m.h[:], m.dinv3, h_table)
        edge_sum(nc, m, h_table, m.src, D, D)
        sums_to_rows(nc, m, D, m.ident[0:D, 0:D], m.cur, D)
        add_bias(nc, m, m.cur[:], m.b3[:], scale=m.dinv3)
        layer_norm(nc, m, m.cur[:], out)


def kernel(**inputs):
    import numpy as _np
    import concourse.bacc as _bacc
    from concourse import mybir as _mybir
    from concourse.bass_utils import run_bass_kernel_spmd as _run

    v = {k: _np.asarray(x) for k, x in inputs.items()}

    def by_tile(x):
        out = _np.zeros((ET * P,), x.dtype)
        out[:E] = x.reshape(-1)
        return _np.ascontiguousarray(out.reshape(ET, P).T)

    x = _np.zeros((NP, D), v["x"].dtype)
    x[:N] = v["x"]
    w1 = v["L2_gnn_W1"]
    laid = {
        "x": x, "xT": x.T, "src": by_tile(v["src"]), "dst": by_tile(v["dst"]), "rel": by_tile(v["edge_type_32"]),
        "attr": by_tile(v["edge_weight1"]), "w0": v["L0_gnn_weight"].transpose(1, 0, 2).reshape(D, R * D),
        "w1": v["L1_gnn_Ws"].transpose(1, 0, 2), "b1": v["L1_gnn_bs"], "wout": v["L1_gnn_W_out"],
        "bout": v["L1_gnn_b_out"], "wa": w1[:, :D].T, "wb": w1[:, D:2 * D].T, "wc": w1[:, 2 * D],
        "bh": v["L2_gnn_b1"], "w2": v["L2_gnn_W2"].T, "b2": v["L2_gnn_b2"], "wih": v["L2_gnn_W_ih"].T,
        "whh": v["L2_gnn_W_hh"].T, "bih": v["L2_gnn_b_ih"], "bhh": v["L2_gnn_b_hh"], "w3": v["L3_gnn_weight"],
        "b3": v["L3_gnn_bias"],
    }
    nc = _bacc.Bacc("TRN2", target_bir_lowering=False, num_devices=1)
    arrays, a = {}, {}
    for name, x in laid.items():
        x = _np.ascontiguousarray(x)
        arrays[f"in_{name}"] = x
        a[name] = nc.dram_tensor(f"in_{name}", x.shape, _mybir.dt.from_np(x.dtype), kind="ExternalInput").ap()
    out = nc.dram_tensor("out_x", (N, D), _mybir.dt.float32, kind="ExternalOutput").ap()
    build(nc, a, out)
    r = _run(nc, [arrays], core_ids=[0])
    return r.results[0]["out_x"]
```

```python
import concourse.bass as bass
import numpy as np
from concourse import mybir
from concourse.alu_op_type import AluOpType as ALU
from contextlib import ExitStack

F32 = mybir.dt.float32
I32 = mybir.dt.int32
ACT = mybir.ActivationFunctionType
AX = mybir.AxisListType
P = 128
N = 6250
E = 206250
D = 64
HID = 128
R = 32
NB = (N + P - 1) // P
NP = NB * P
ET = (E + P - 1) // P
HALF = 13
RING = 2 * HALF
ITER = ET // RING
assert ITER * RING == ET
EPS = 1e-5
BANK = 512


class Mem:
    pass


def alloc(nc, ctx):
    m = Mem()

    def sb(name, shape, dt=F32):
        return ctx.enter_context(nc.sbuf_tensor(name, shape, dt))

    m.src = sb("src", [P, ET], I32)
    m.dst = sb("dst", [P, ET], I32)
    m.rel = sb("rel", [P, ET], I32)
    m.src_rel = sb("src_rel", [P, ET], I32)
    m.attr = sb("attr", [P, ET])
    m.local = sb("local", [P, ET])
    m.stage = sb("stage", [P, RING], I32)
    m.feat = sb("feat", [P, RING, HID])
    m.onehot = sb("onehot", [P, RING, P])
    m.acc = sb("acc", [P, NP + P])
    m.xT = sb("xT", [D, NP])
    m.x = sb("x", [P, NB, D])
    m.cur = sb("cur", [P, NB, D])
    m.h = sb("h", [P, NB, D])
    m.rows = sb("rows", [P, NB, HID])
    m.tmp = sb("tmp", [P, NB, D])
    m.deg = sb("deg", [P, NB])
    m.dinv1 = sb("dinv1", [P, NB])
    m.dinv3 = sb("dinv3", [P, NB])
    m.st = [sb(f"st{i}", [P, NB]) for i in range(3)]
    m.ident = sb("ident", [P, P])
    m.iota = sb("iota", [P, P])
    m.iota_p = sb("iota_p", [P, 1])
    m.ones = sb("ones", [1, P])
    m.w0 = sb("w0", [D, R * D])
    m.w1 = sb("w1", [D, 3, D])
    m.wout = sb("wout", [D, D])
    m.b1 = sb("b1", [P, 3, D])
    m.bout = sb("bout", [P, D])
    m.wa = sb("wa", [D, HID])
    m.wb = sb("wb", [D, HID])
    m.wc = sb("wc", [P, HID])
    m.bh = sb("bh", [P, HID])
    m.w2 = sb("w2", [HID, D])
    m.b2 = sb("b2", [P, D])
    m.wih = sb("wih", [D, 3 * D])
    m.whh = sb("whh", [D, 3 * D])
    m.bih = sb("bih", [P, 3 * D])
    m.bhh = sb("bhh", [P, 3 * D])
    m.w3 = sb("w3", [D, D])
    m.b3 = sb("b3", [P, D])
    m.ps = ctx.enter_context(nc.psum_tensor("ps", [P, 8, BANK], F32))

    def sem(name):
        return ctx.enter_context(nc.semaphore(name))

    m.landed = [sem(f"landed{u}") for u in range(RING)]
    m.staged = sem("staged")
    m.compared, m.summed, m.added = sem("compared"), sem("summed"), sem("added")
    m.passes = 0
    m.multiplied = sem("multiplied")
    m.copied = [sem("dve_copied"), sem("act_copied")]
    m.groups, m.copies = 0, [0, 0]
    return m


def load(nc, m, a):
    with nc.semaphore("loaded") as loaded, nc.semaphore("iotas") as iotas, nc.semaphore("ready") as ready, \
            nc.semaphore("based") as based, nc.semaphore("ident_zero") as ident_zero, nc.Block() as block:
        row_bias = [(m.bout, "bout"), (m.bh, "bh"), (m.b2, "b2"), (m.bih, "bih"), (m.bhh, "bhh"), (m.b3, "b3"),
                    (m.wc, "wc")]
        plain = [(m.src, "src"), (m.dst, "dst"), (m.rel, "rel"), (m.attr, "attr"), (m.xT, "xT"), (m.w0, "w0"),
                 (m.w1, "w1"), (m.wout, "wout"), (m.wa, "wa"), (m.wb, "wb"), (m.w2, "w2"), (m.wih, "wih"),
                 (m.whh, "whh"), (m.w3, "w3")]
        total = 16 * (len(row_bias) + len(plain) + 2)

        @block.sync
        def _(sp):
            for t, name in plain:
                sp.dma_start(t[:], a[name]).then_inc(loaded, 16)
            sp.dma_start(m.x[:], a["x"].rearrange("(b p) d -> p b d", p=P)).then_inc(loaded, 16)
            for t, name in row_bias:
                sp.dma_start(t[:], a[name].partition_broadcast(P)).then_inc(loaded, 16)
            sp.dma_start(m.b1[:], a["b1"].partition_broadcast(P)).then_inc(loaded, 16)

        @block.gpsimd
        def _(pool):
            pool.iota(m.iota[:], [[1, P]], base=0, channel_multiplier=0,
                      allow_small_or_imprecise_dtypes=True).then_inc(iotas, 1)
            pool.iota(m.iota_p[:], [[1, 1]], base=0, channel_multiplier=1,
                      allow_small_or_imprecise_dtypes=True).then_inc(iotas, 1)
            pool.memset(m.ident[:], 0.0).then_inc(ident_zero, 1)
            pool.wait_ge(ident_zero, 1)
            pool.affine_select(out=m.ident[:], in_=m.ident[:], compare_op=ALU.not_equal, fill=1.0, base=0,
                               pattern=[[-1, P]], channel_multiplier=1).then_inc(iotas, 1)

        @block.tensor
        def _(pe):
            pe.wait_ge(ready, 3)
            for c in range(4):
                w = ET // 4
                nc.tensor.matmul(m.ps[:, c, 0:w], m.ones[:], m.tmp[0:1, :, :].rearrange("p b d -> p (b d)")[:, c * w:(c + 1) * w],
                                 start=True, stop=True).then_inc(based, 1)

        @block.vector
        def _(dve):
            dve.memset(m.ones[:], 1.0).then_inc(ready, 1)
            dve.memset(m.feat[:], 1.0)
            dve.wait_ge(loaded, total)
            dve.tensor_copy(m.tmp[0:1, :, :].rearrange("p b d -> p (b d)")[:, 0:ET], m.dst[0:1, :]).then_inc(ready, 1)
            dve.scalar_tensor_tensor(m.src_rel[:], m.src[:], float(R), m.rel[:], op0=ALU.mult, op1=ALU.add)
            dve.tensor_copy(m.local[:], m.dst[:]).then_inc(ready, 1)
            dve.wait_ge(ready, 3)
            dve.wait_ge(based, 4)
            w = ET // 4
            for c in range(4):
                dve.tensor_tensor(m.local[:, c * w:(c + 1) * w], m.local[:, c * w:(c + 1) * w], m.ps[:, c, 0:w],
                                  ALU.subtract)

        @block.scalar
        def _(act):
            act.wait_ge(iotas, 3)
            act.wait_ge(loaded, total)


def relation_table(nc, m, table):
    y = m.rows[:, 0:2 * R * D // HID, :].rearrange("p b d -> p (b d)").rearrange("p (k c) -> p k c", k=2)
    with nc.semaphore("rel_multiplied") as multiplied, \
            nc.semaphore("rel_act_copied") as act_copied, nc.semaphore("rel_dve_copied") as dve_copied, \
            nc.semaphore("stored0") as stored0, nc.semaphore("stored1") as stored1, nc.Block() as block:
        stored = [stored0, stored1]
        t = table.rearrange("(n r) d -> n (r d)", r=R)
        half = R * D // 2

        @block.tensor
        def _(pe):
            for b in range(NB):
                if b >= 2:
                    pe.wait_ge(act_copied, b - 1)
                    pe.wait_ge(dve_copied, b - 1)
                for q in range(4):
                    k = nc.tensor.matmul(m.ps[:, 4 * (b % 2) + q, :], m.xT[:, b * P:(b + 1) * P],
                                         m.w0[:, q * BANK:(q + 1) * BANK], start=True, stop=True)
                k.then_inc(multiplied, 1)

        def copy(e, b, copied, lo):
            e.wait_ge(multiplied, b + 1)
            if b >= 2:
                e.wait_ge(stored[b % 2], 16 * (b // 2))
            o = y[:, b % 2, lo * half:(lo + 1) * half]
            i = m.ps[:, 4 * (b % 2) + 2 * lo:4 * (b % 2) + 2 * lo + 2, :].rearrange("p q c -> p (q c)")
            (e.copy(o, i) if lo else e.tensor_copy(o, i)).then_inc(copied, 1)

        @block.vector
        def _(dve):
            for b in range(NB):
                copy(dve, b, dve_copied, 0)

        @block.scalar
        def _(act):
            for b in range(NB):
                copy(act, b, act_copied, 1)

        @block.sync
        def _(sp):
            for b in range(NB):
                sp.wait_ge(act_copied, b + 1)
                sp.wait_ge(dve_copied, b + 1)
                sp.dma_start(t[b * P:(b + 1) * P, :], y[:, b % 2, :]).then_inc(stored[b % 2], 16)
            for i in range(2):
                sp.wait_ge(stored[i], 16 * ((NB + 1 - i) // 2))


def window_starts(nc, m, engine, i, u):
    if u % HALF == 0:
        _, m.starts = nc.values_load_multi_w_load_instructions(
            m.dst[0:1, bass.ds(i * RING + u, HALF)], engines=(engine.engine,), min_val=0, max_val=N - 1,
            skip_runtime_bounds_check_because="a destination is one of the N nodes")
    return m.starts[u % HALF]


def edge_sum(nc, m, table, index, width, rows):
    with ExitStack() as ctx:
        cleared = ctx.enter_context(nc.semaphore("cleared"))
        landed, staged, compared, summed, added = m.landed, m.staged, m.compared, m.summed, m.added
        tiles0, iters0 = m.passes * ET, m.passes * ITER
        m.passes += 1
        block = ctx.enter_context(nc.Block())

        @block.scalar
        def _(act):
            def stage(i, first):
                for h in range(2):
                    if not first:
                        act.wait_ge(summed, tiles0 + RING * (i - 1) + HALF * (h + 1))
                    act.copy(m.stage[:, h * HALF:(h + 1) * HALF],
                             index[:, bass.ds(i * RING + h * HALF, HALF)]).then_inc(staged, 1)
            stage(0, True)
            with act.Fori(1, ITER) as i:
                stage(i, False)

        @block.gpsimd
        def _(pool):
            def gather(i):
                for u in range(RING):
                    if u % HALF == 0:
                        pool.wait_ge(staged, 2 * iters0 + 2 * i + u // HALF + 1)
                        pool.nop(nofuse=True)
                    pool.indirect_dma_start(m.feat[:, u, 0:width], None, table,
                                            bass.IndirectOffsetOnAxis(ap=m.stage[:, u:u + 1], axis=0)
                                            ).then_inc(landed[u], 16)
            gather(0)
            with pool.Fori(1, ITER) as i:
                gather(i)

        @block.tensor
        def _(pe):
            def tiles(i, first):
                for u in range(RING):
                    pe.wait_ge(landed[u], 16 * iters0 + 16 * i + 16)
                    pe.wait_ge(compared, tiles0 + RING * i + u + 1)
                    if not (first and u < 2):
                        pe.wait_ge(added, tiles0 + RING * i + u - 1)
                    nc.tensor.matmul(m.ps[0:rows, u % 2, 0:P], m.feat[:, u, 0:rows], m.onehot[:, u, :],
                                     start=True, stop=True).then_inc(summed, 1)
            tiles(0, True)
            with pe.Fori(1, ITER) as i:
                tiles(i, False)

        @block.vector
        def _(dve):
            def compare(i, u):
                dve.tensor_scalar(m.onehot[:, u, :], m.iota[:], m.local[:, bass.ds(i * RING + u, 1)], None,
                                  ALU.is_equal).then_inc(compared, 1)

            def add(i, u, first):
                base = window_starts(nc, m, dve, i, u)
                dve.wait_ge(summed, tiles0 + RING * i + u + 1)
                if not (first and u == 0):
                    dve.wait_ge(added, tiles0 + RING * i + u)
                window = m.acc[0:rows, bass.ds(base, P)]
                dve.tensor_tensor(window, window, m.ps[0:rows, u % 2, 0:P], ALU.add).then_inc(added, 1)

            dve.memset(m.acc[0:rows, :], 0.0).then_inc(cleared, 1)
            for u in range(RING):
                compare(0, u)
            dve.wait_ge(cleared, 1)

            def tiles(i, first):
                for u in range(RING):
                    add(i, u, first)
                    compare(i + 1, u)
            tiles(0, True)
            with dve.Fori(1, ITER - 1) as i:
                tiles(i, False)
            for u in range(RING):
                add(ITER - 1, u, False)


def edge_mlp_sum(nc, m, table, q):
    with ExitStack() as ctx:
        sem = lambda name: ctx.enter_context(nc.semaphore(name))
        landed, staged, compared, summed, added = m.landed, m.staged, m.compared, m.summed, m.added
        tiles0, iters0 = m.passes * ET, m.passes * ITER
        m.passes += 1
        fetched = [sem(f"fetched{u}") for u in range(HALF)]
        names = ("cleared", "spread", "turned", "hidden", "biased", "activated")
        cleared, spread, turned, hidden, biased, activated = map(sem, names)
        flat = m.h[:].rearrange("p b d -> p (b d)").rearrange("p (k c) -> p k c", c=HID) if NB % 2 == 0 else \
            m.h[:, 0:NB - 1, :].rearrange("p (k two) d -> p k (two d)", two=2)
        other = m.tmp[:, 0:NB - 1, :].rearrange("p (k two) d -> p k (two d)", two=2)
        window_q = flat[:, 0:HALF, :]
        turned_hot = other[:, 0:2, :]
        act_in = other[:, 2:4, :]
        act_out = other[:, 4:6, :]
        block = ctx.enter_context(nc.Block())

        def wait(e, sem, count, so_far=0):
            if not isinstance(count, int) or count > 0:
                e.wait_ge(sem, so_far + count)


        @block.scalar
        def _(act):
            def stage(i, h):
                act.copy(m.stage[:, h * HALF:(h + 1) * HALF],
                         m.src[:, bass.ds(i * RING + h * HALF, HALF)]).then_inc(staged, 1)

            def turn(i, u):
                g = i * RING + u
                act.wait_ge(spread, g + 1)
                wait(act, hidden, g - 1)
                act.copy(turned_hot[:, u % 2, :], m.ps[:, 2 + u % 2, 0:P]).then_inc(turned, 1)

            def relu(i, u):
                g = i * RING + u
                act.wait_ge(hidden, g + 1)
                wait(act, summed, g - 1, tiles0)
                act.activation(act_out[:, u % 2, :], m.ps[:, 4 + u % 2, 0:HID], ACT.Relu).then_inc(activated, 1)

            def steps(i, last):
                for u in range(RING):
                    if not last or u + 2 < RING:
                        turn(i, u + 2)
                    if not last or u + 1 < RING:
                        relu(i, u + 1)
                    if (u + 1) % HALF == HALF - 1 and not last:
                        stage(i + 1, u // HALF)

            for h in range(2):
                stage(0, h)
            turn(0, 0)
            turn(0, 1)
            relu(0, 0)
            steps(0, False)
            with act.Fori(1, ITER - 1) as i:
                steps(i, False)
            steps(ITER - 1, True)

        @block.gpsimd
        def _(pool):
            def gather(i):
                for u in range(RING):
                    if u % HALF == 0:
                        pool.wait_ge(staged, 2 * iters0 + 2 * i + u // HALF + 1)
                        pool.nop(nofuse=True)
                    pool.indirect_dma_start(m.feat[:, u, :], None, table,
                                            bass.IndirectOffsetOnAxis(ap=m.stage[:, u:u + 1], axis=0)
                                            ).then_inc(landed[u], 16)
            gather(0)
            with pool.Fori(1, ITER) as i:
                gather(i)

        @block.sync
        def _(sp):
            def fetch(i):
                for u in range(RING):
                    g = i * RING + u
                    base = window_starts(nc, m, sp, i, u)
                    wait(sp, hidden, g + 1 - HALF)
                    sp.dma_start(window_q[:, u % HALF, :], q[bass.ds(base, P), :]).then_inc(fetched[u % HALF], 16)
            fetch(0)
            with sp.Fori(1, ITER) as i:
                fetch(i)

        @block.tensor
        def _(pe):
            def turn(i, u):
                g = i * RING + u
                pe.wait_ge(compared, tiles0 + g + 1)
                wait(pe, turned, g - 1)
                nc.tensor.transpose(m.ps[:, 2 + u % 2, 0:P], m.onehot[:, u % RING, :], m.ident[:]).then_inc(spread, 1)

            def hide(i, u):
                g = i * RING + u
                wait(pe, activated, g - 1)
                pe.wait_ge(biased, g + 1)
                nc.tensor.matmul(m.ps[:, 4 + u % 2, 0:HID], m.ident[:], act_in[:, u % 2, :], start=True, stop=False)
                pe.wait_ge(turned, g + 1)
                pe.wait_ge(fetched[u % HALF], 32 * i + 16 * (u // HALF) + 16)
                nc.tensor.matmul(m.ps[:, 4 + u % 2, 0:HID], turned_hot[:, u % 2, :], window_q[:, u % HALF, :],
                                 start=False, stop=True).then_inc(hidden, 1)

            def total(i, u):
                g = i * RING + u
                wait(pe, added, g - 1, tiles0)
                pe.wait_ge(activated, g + 1)
                nc.tensor.matmul(m.ps[:, u % 2, 0:P], act_out[:, u % 2, :], m.onehot[:, u, :], start=True,
                                 stop=True).then_inc(summed, 1)

            def steps(i, last):
                for u in range(RING):
                    if not last or u + 2 < RING:
                        turn(i, u + 2)
                    if not last or u + 1 < RING:
                        hide(i, u + 1)
                    total(i, u)

            turn(0, 0)
            turn(0, 1)
            hide(0, 0)
            steps(0, False)
            with pe.Fori(1, ITER - 1) as i:
                steps(i, False)
            steps(ITER - 1, True)

        @block.vector
        def _(dve):
            def compare(i, u):
                dve.tensor_scalar(m.onehot[:, u, :], m.iota[:], m.local[:, bass.ds(i * RING + u, 1)], None,
                                  ALU.is_equal).then_inc(compared, 1)

            def bias(i, u):
                g = i * RING + u
                dve.wait_ge(landed[u % RING], 16 * iters0 + 16 * i + 16 * (u // RING) + 16)
                wait(dve, hidden, g - 1)
                dve.scalar_tensor_tensor(act_in[:, u % 2, :], m.wc[:], m.attr[:, bass.ds(g, 1)],
                                         m.feat[:, u % RING, :], op0=ALU.mult, op1=ALU.add).then_inc(biased, 1)

            def add(i, u):
                g = i * RING + u
                base = window_starts(nc, m, dve, i, u)
                dve.wait_ge(summed, tiles0 + g + 1)
                wait(dve, added, g, tiles0)
                window = m.acc[:, bass.ds(base, P)]
                dve.tensor_tensor(window, window, m.ps[:, u % 2, 0:P], ALU.add).then_inc(added, 1)

            def steps(i, last):
                for u in range(RING):
                    if not last or u + 2 < RING:
                        bias(i, u + 2)
                    add(i, u)
                    if not last:
                        compare(i + 1, u)

            dve.memset(m.acc[:], 0.0).then_inc(cleared, 1)
            for u in range(RING):
                compare(0, u)
            bias(0, 0)
            bias(0, 1)
            dve.wait_ge(cleared, 1)
            steps(0, False)
            with dve.Fori(1, ITER - 1) as i:
                steps(i, False)
            steps(ITER - 1, True)


def products(nc, m, name, width, per_bank, operands, dest):
    groups = [range(g, min(g + per_bank, NB)) for g in range(0, NB, per_bank)]
    multiplied, copied = m.multiplied, m.copied
    groups0, copies0 = m.groups, list(m.copies)
    m.groups += len(groups)
    m.copies = [copies0[k] + (len(groups) + 1 - k) // 2 for k in range(2)]
    with nc.Block() as block:
        @block.tensor
        def _(pe):
            for g, blocks in enumerate(groups):
                if g >= 8:
                    pe.wait_ge(copied[g % 2], copies0[g % 2] + (g - 8) // 2 + 1)
                for j, b in enumerate(blocks):
                    pairs = operands(b)
                    for k, (w, x) in enumerate(pairs):
                        last = nc.tensor.matmul(m.ps[0:w.shape[1], g % 8, j * width:(j + 1) * width], w, x,
                                                start=k == 0, stop=k == len(pairs) - 1)
                last.then_inc(multiplied, 1)

        def copy(e, g, put):
            blocks = groups[g]
            e.wait_ge(multiplied, groups0 + g + 1)
            rows = operands(0)[0][0].shape[1]
            put(dest(blocks[0], len(blocks)), m.ps[0:rows, g % 8, 0:len(blocks) * width]).then_inc(copied[g % 2], 1)

        @block.vector
        def _(dve):
            for g in range(0, len(groups), 2):
                copy(dve, g, dve.tensor_copy)

        @block.scalar
        def _(act):
            for g in range(1, len(groups), 2):
                copy(act, g, act.copy)


def transpose_rows(nc, m, rows, out=None):
    out = m.xT if out is None else out
    products(nc, m, "turn", P, 4, lambda b: [(rows[:, b, :], m.ident[:])],
             lambda b, n: out[:, b * P:(b + n) * P])


def project(nc, m, w, out, width):
    per = BANK // width
    products(nc, m, "project", width, per, lambda b: [(m.xT[:, b * P:(b + 1) * P], w)],
             lambda b, n: out[:, b:b + n, 0:width].rearrange("p b d -> p (b d)") if out.shape[2] == width
             else out[:, b:b + n, 0:width])


def sums_to_rows(nc, m, k, w, out, width):
    products(nc, m, "sums", width, BANK // width, lambda b: [(m.acc[0:k, b * P:(b + 1) * P], w)],
             lambda b, n: out[:, b:b + n, 0:width])


def per_node(t):
    return t[:, :].unsqueeze(2).broadcast_to([P, NB, D])


def per_feature(t, width=D):
    return t.unsqueeze(1).broadcast_to([P, NB, width])


def layer_norm(nc, m, update, out_dram=None):
    total, mean, rstd = m.st
    with nc.semaphore("step") as step, nc.semaphore("stored") as stored, nc.Block() as block:
        @block.vector
        def _(dve):
            dve.tensor_tensor(m.x[:], m.x[:], update, ALU.add).then_inc(step, 1)
            dve.wait_ge(step, 1)
            dve.tensor_reduce(total[:], m.x[:], axis=AX.X, op=ALU.add).then_inc(step, 1)
            dve.wait_ge(step, 2)
            dve.tensor_scalar(mean[:], total[:], 1.0 / D, None, ALU.mult).then_inc(step, 1)
            dve.wait_ge(step, 3)
            dve.tensor_tensor(m.x[:], m.x[:], per_node(mean), ALU.subtract).then_inc(step, 1)
            dve.wait_ge(step, 5)
            dve.tensor_reduce(total[:], m.tmp[:], axis=AX.X, op=ALU.add).then_inc(step, 1)
            dve.wait_ge(step, 6)
            dve.tensor_scalar(total[:], total[:], 1.0 / D, EPS, ALU.mult, ALU.add).then_inc(step, 1)
            dve.wait_ge(step, 8)
            dve.reciprocal(rstd[:], mean[:]).then_inc(step, 1)
            dve.wait_ge(step, 9)
            dve.tensor_tensor(m.x[:], m.x[:], per_node(rstd), ALU.mult).then_inc(step, 1)

        @block.scalar
        def _(act):
            act.wait_ge(step, 4)
            act.activation(m.tmp[:], m.x[:], ACT.Square).then_inc(step, 1)
            act.wait_ge(step, 7)
            act.activation(mean[:], total[:], ACT.Sqrt).then_inc(step, 1)

        if out_dram is not None:
            @block.sync
            def _(sp):
                sp.wait_ge(step, 10)
                full = N // P
                sp.dma_start(out_dram[0:full * P, :].rearrange("(b p) d -> p b d", p=P),
                             m.x[:, 0:full, :]).then_inc(stored, 16)
                sp.dma_start(out_dram[full * P:N, :], m.x[0:N - full * P, full, :]).then_inc(stored, 16)
                sp.wait_ge(stored, 32)


def degrees(nc, m):
    with nc.semaphore("step") as step, nc.Block() as block:
        @block.vector
        def _(dve):
            dve.tensor_copy(m.deg[:], m.rows[:, :, D]).then_inc(step, 1)
            dve.wait_ge(step, 1)
            dve.tensor_scalar(m.st[0][:], m.deg[:], 1.0, None, ALU.add).then_inc(step, 1)
            dve.tensor_scalar(m.st[1][:], m.deg[:], 1.0, None, ALU.max).then_inc(step, 1)
            dve.wait_ge(step, 5)
            dve.reciprocal(m.dinv1[:], m.st[2][:]).then_inc(step, 1)
            dve.reciprocal(m.st[0][:], m.dinv3[:]).then_inc(step, 1)
            dve.wait_ge(step, 7)
            dve.scalar_tensor_tensor(m.dinv3[:], m.deg[:], 0.0, m.st[0][:], op0=ALU.is_gt, op1=ALU.mult)

        @block.scalar
        def _(act):
            act.wait_ge(step, 3)
            act.activation(m.st[2][:], m.st[0][:], ACT.Sqrt).then_inc(step, 1)
            act.activation(m.dinv3[:], m.st[1][:], ACT.Sqrt).then_inc(step, 1)


def scale_and_store(nc, m, rows, scale, table, bias=None, width=D):
    with nc.semaphore("scaled") as scaled, nc.semaphore("stored") as stored, nc.Block() as block:
        @block.vector
        def _(dve):
            if scale is not None:
                dve.tensor_tensor(rows, rows, per_node(scale), ALU.mult).then_inc(scaled, 1)
            if bias is not None:
                dve.tensor_tensor(rows, rows, per_feature(bias, width), ALU.add).then_inc(scaled, 1)

        @block.sync
        def _(sp):
            if scale is not None or bias is not None:
                sp.wait_ge(scaled, 1)
            sp.dma_start(table[0:NP, :].rearrange("(b p) d -> p b d", p=P), rows).then_inc(stored, 16)
            sp.wait_ge(stored, 16)


def gcn_finish(nc, m, bias):
    r = m.rows[:, :, 0:D]
    with nc.semaphore("step") as step, nc.Block() as block:
        @block.vector
        def _(dve):
            dve.tensor_tensor(m.cur[:], r, m.h[:], ALU.add).then_inc(step, 1)
            dve.wait_ge(step, 1)
            dve.tensor_tensor(m.cur[:], m.cur[:], per_node(m.dinv1), ALU.mult).then_inc(step, 1)
            dve.wait_ge(step, 2)
            dve.tensor_tensor(m.cur[:], m.cur[:], per_feature(bias), ALU.add).then_inc(step, 1)
            dve.wait_ge(step, 3)
            dve.tensor_scalar(m.cur[:], m.cur[:], 0.0, None, ALU.max)


def add_bias(nc, m, rows, bias, scale=None, by_degree=False):
    with nc.semaphore("step") as step, nc.Block() as block:
        @block.vector
        def _(dve):
            if scale is not None:
                dve.tensor_tensor(rows, rows, per_node(scale), ALU.mult).then_inc(step, 1)
                dve.wait_ge(step, 1)
            if by_degree:
                dve.tensor_tensor(m.tmp[:], per_feature(bias), per_node(m.deg), ALU.mult).then_inc(step, 1)
                dve.wait_ge(step, 1)
                dve.tensor_tensor(rows, rows, m.tmp[:], ALU.add)
            else:
                dve.tensor_tensor(rows, rows, per_feature(bias), ALU.add)


def gru(nc, m, aggrT):
    r, z, n = m.h, m.tmp, m.rows
    rz = lambda lo: (m.bih[:, lo:lo + D], m.bhh[:, lo:lo + D])
    for lo, out in ((0, r), (D, z)):
        products(nc, m, "gate", D, 8, lambda b: [(aggrT[:, b * P:(b + 1) * P], m.wih[:, lo:lo + D]),
                                                (m.xT[:, b * P:(b + 1) * P], m.whh[:, lo:lo + D])],
                 lambda b, k: out[:, b:b + k, :].rearrange("p b d -> p (b d)"))
    products(nc, m, "new_in", D, 8, lambda b: [(aggrT[:, b * P:(b + 1) * P], m.wih[:, 2 * D:3 * D])],
             lambda b, k: n[:, b:b + k, 0:D])
    products(nc, m, "new_state", D, 8, lambda b: [(m.xT[:, b * P:(b + 1) * P], m.whh[:, 2 * D:3 * D])],
             lambda b, k: n[:, b:b + k, D:2 * D])
    i_n, h_n = n[:, :, 0:D], n[:, :, D:2 * D]
    with nc.semaphore("step") as step, nc.Block() as block:
        @block.vector
        def _(dve):
            at = 0
            for lo, g in ((0, r), (D, z)):
                for b in rz(lo):
                    if at:
                        dve.wait_ge(step, at)
                    dve.tensor_tensor(g[:], g[:], per_feature(b), ALU.add).then_inc(step, 1)
                    at += 1
            for part, b in ((i_n, m.bih), (h_n, m.bhh)):
                dve.tensor_tensor(part, part, per_feature(b[:, 2 * D:3 * D]), ALU.add).then_inc(step, 1)
            dve.wait_ge(step, 8)
            dve.tensor_tensor(h_n, h_n, r[:], ALU.mult).then_inc(step, 1)
            dve.wait_ge(step, 9)
            dve.tensor_tensor(h_n, h_n, i_n, ALU.add).then_inc(step, 1)
            dve.wait_ge(step, 11)
            dve.tensor_tensor(m.cur[:], m.x[:], h_n, ALU.subtract).then_inc(step, 1)
            dve.wait_ge(step, 12)
            dve.tensor_tensor(m.cur[:], m.cur[:], z[:], ALU.mult).then_inc(step, 1)
            dve.wait_ge(step, 13)
            dve.tensor_tensor(m.cur[:], m.cur[:], h_n, ALU.add)

        @block.scalar
        def _(act):
            act.wait_ge(step, 6)
            act.activation(r[:], r[:], ACT.Sigmoid).then_inc(step, 1)
            act.activation(z[:], z[:], ACT.Sigmoid).then_inc(step, 1)
            act.wait_ge(step, 10)
            act.activation(h_n, h_n, ACT.Tanh).then_inc(step, 1)


def build(nc, a, out):
    rel_table = nc.dram_tensor("rel_table", (NP * R, D), F32).ap()
    h_table = nc.dram_tensor("h_table", (NP, D), F32).ap()
    p_table = nc.dram_tensor("p_table", (NP, HID), F32).ap()
    q_table = nc.dram_tensor("q_table", (NP + P, HID), F32).ap()
    with ExitStack() as ctx:
        m = alloc(nc, ctx)
        load(nc, m, a)
        relation_table(nc, m, rel_table)
        edge_sum(nc, m, rel_table, m.src_rel, D, D + 1)
        sums_to_rows(nc, m, D + 1, m.ident[0:D + 1, 0:D + 1], m.rows, D + 1)
        degrees(nc, m)
        layer_norm(nc, m, m.rows[:, :, 0:D])
        for i in range(3):
            transpose_rows(nc, m, m.cur if i else m.x)
            project(nc, m, m.w1[:, i, :], m.h, D)
            scale_and_store(nc, m, m.h[:], m.dinv1, h_table)
            edge_sum(nc, m, h_table, m.src, D, D)
            sums_to_rows(nc, m, D, m.ident[0:D, 0:D], m.rows, D)
            gcn_finish(nc, m, m.b1[:, i, :])
        transpose_rows(nc, m, m.cur)
        project(nc, m, m.wout[:], m.h, D)
        add_bias(nc, m, m.h[:], m.bout[:])
        layer_norm(nc, m, m.h[:])
        transpose_rows(nc, m, m.x)
        project(nc, m, m.wa[:], m.rows, HID)
        scale_and_store(nc, m, m.rows[:], None, p_table)
        project(nc, m, m.wb[:], m.rows, HID)
        scale_and_store(nc, m, m.rows[:], None, q_table, bias=m.bh[:], width=HID)
        with nc.semaphore("padded") as padded, nc.Block() as block:
            @block.sync
            def _(sp):
                sp.dma_start(q_table[NP:NP + P, :], m.ident[:]).then_inc(padded, 16)
                sp.wait_ge(padded, 16)
        edge_mlp_sum(nc, m, p_table, q_table)
        sums_to_rows(nc, m, HID, m.w2[:], m.cur, D)
        add_bias(nc, m, m.cur[:], m.b2[:], by_degree=True)
        transpose_rows(nc, m, m.cur, m.acc[0:D, 0:NP])
        gru(nc, m, m.acc[0:D, 0:NP])
        layer_norm(nc, m, m.cur[:])
        transpose_rows(nc, m, m.x)
        project(nc, m, m.w3[:], m.h, D)
        scale_and_store(nc, m, m.h[:], m.dinv3, h_table)
        edge_sum(nc, m, h_table, m.src, D, D)
        sums_to_rows(nc, m, D, m.ident[0:D, 0:D], m.cur, D)
        add_bias(nc, m, m.cur[:], m.b3[:], scale=m.dinv3)
        layer_norm(nc, m, m.cur[:], out)


def kernel(**inputs):
    import numpy as _np
    import concourse.bacc as _bacc
    from concourse import mybir as _mybir
    from concourse.bass_utils import run_bass_kernel_spmd as _run

    v = {k: _np.asarray(x) for k, x in inputs.items()}

    def by_tile(x):
        out = _np.zeros((ET * P,), x.dtype)
        out[:E] = x.reshape(-1)
        return _np.ascontiguousarray(out.reshape(ET, P).T)

    x = _np.zeros((NP, D), v["x"].dtype)
    x[:N] = v["x"]
    w1 = v["L2_gnn_W1"]
    laid = {
        "x": x, "xT": x.T, "src": by_tile(v["src"]), "dst": by_tile(v["dst"]), "rel": by_tile(v["edge_type_32"]),
        "attr": by_tile(v["edge_weight1"]), "w0": v["L0_gnn_weight"].transpose(1, 0, 2).reshape(D, R * D),
        "w1": v["L1_gnn_Ws"].transpose(1, 0, 2), "b1": v["L1_gnn_bs"], "wout": v["L1_gnn_W_out"],
        "bout": v["L1_gnn_b_out"], "wa": w1[:, :D].T, "wb": w1[:, D:2 * D].T, "wc": w1[:, 2 * D],
        "bh": v["L2_gnn_b1"], "w2": v["L2_gnn_W2"].T, "b2": v["L2_gnn_b2"], "wih": v["L2_gnn_W_ih"].T,
        "whh": v["L2_gnn_W_hh"].T, "bih": v["L2_gnn_b_ih"], "bhh": v["L2_gnn_b_hh"], "w3": v["L3_gnn_weight"],
        "b3": v["L3_gnn_bias"],
    }
    nc = _bacc.Bacc("TRN2", target_bir_lowering=False, num_devices=1)
    arrays, a = {}, {}
    for name, x in laid.items():
        x = _np.ascontiguousarray(x)
        arrays[f"in_{name}"] = x
        a[name] = nc.dram_tensor(f"in_{name}", x.shape, _mybir.dt.from_np(x.dtype), kind="ExternalInput").ap()
    out = nc.dram_tensor("out_x", (N, D), _mybir.dt.float32, kind="ExternalOutput").ap()
    build(nc, a, out)
    r = _run(nc, [arrays], core_ids=[0])
    return r.results[0]["out_x"]
```

```python
import concourse.bass as bass
import numpy as np
from concourse import mybir
from concourse.alu_op_type import AluOpType as ALU
from contextlib import ExitStack

F32 = mybir.dt.float32
I32 = mybir.dt.int32
F16 = mybir.dt.float16
BF16 = mybir.dt.bfloat16
ACT = mybir.ActivationFunctionType
AX = mybir.AxisListType
P = 128
N = 6250
E = 206250
D = 64
HID = 128
R = 32
NB = (N + P - 1) // P
NP = NB * P
ET = (E + P - 1) // P
HALF = 13
RING = 2 * HALF
ITER = ET // RING
assert ITER * RING == ET
EPS = 1e-5
BANK = 512
WIN = 8
WT = 4
ACT_TILES = 2
NW = NP // WIN
KEYS = WIN * NB
CHUNK = BANK
NC = (NP + CHUNK - 1) // CHUNK
TAIL = NP - (NC - 1) * CHUNK
PIECE = 7
NPIECE = NB // PIECE
assert NPIECE * PIECE == NB and NW * WIN == NP and WT * P <= 2048
GROUP = P // WIN
THIRD = 11
RING0 = 3 * THIRD
LAST0 = ET - (NB - 1) * RING0
assert 2 * THIRD < LAST0 <= RING0


class Mem:
    pass


def edge_semaphores(sem, name, slots):
    s = Mem()
    s.landed = [sem(f"{name}landed{u}") for u in range(slots)]
    s.staged = sem(name + "staged")
    s.compared, s.summed, s.added = sem(name + "compared"), sem(name + "summed"), sem(name + "added")
    s.cleared = sem(name + "cleared")
    s.passes = s.landings = s.stagings = s.clearings = 0
    return s


def edge_buffers(flat):
    feat = flat[:, 0:RING * HID].rearrange("p (u d) -> p u d", u=RING)
    onehot = flat[:, RING * HID:RING * (HID + P)].rearrange("p (u d) -> p u d", u=RING)
    return feat, onehot, flat[:, RING * (HID + P):RING * (HID + P + 1)].bitcast(I32)


def alloc(nc, ctx):
    m = Mem()

    def sb(name, shape, dt=F32):
        return ctx.enter_context(nc.sbuf_tensor(name, shape, dt))

    m.src = sb("src", [P, ET], I32)
    m.dst = sb("dst", [P, ET], I32)
    m.rel = sb("rel", [P, ET], I32)
    m.src_rel = sb("src_rel", [P, NB * RING0], I32)
    m.attr = sb("attr", [P, ET])
    m.key = m.attr
    m.lo = m.rel[:].bitcast(F32)
    m.local = sb("local", [P, ET])
    m.key_iota = sb("key_iota", [P, KEYS], F16)
    m.lo_iota = sb("lo_iota", [P, P], BF16)
    m.lo_off = sb("lo_off", [P, 2, ACT_TILES, P], BF16)
    m.window_tile = sb("window_tile", [1, (NW + P - 1) // P * P], I32)
    m.pick = sb("pick", [P, GROUP, WT])
    store = sb("store", [P, RING * (HID + P + 1)])
    m.feat, m.onehot, m.stage = edge_buffers(store)
    m.sum_rows = store[:, 0:NB * D].rearrange("p (b d) -> p b d", d=D)
    at = 0

    def part(columns):
        nonlocal at
        at += columns
        return store[:, at - columns:at]

    m.feat0 = part(RING0 * (D + 1)).rearrange("p (u d) -> p u d", u=RING0)
    m.onehot0 = part(THIRD * P).rearrange("p (u d) -> p u d", u=THIRD)
    m.stage0 = part(RING0).bitcast(I32)
    m.keys = part(WT * KEYS).bitcast(F16).rearrange("p (k j n) -> p k j n", k=2, j=WT)
    m.los = part(WT * P).bitcast(BF16).rearrange("p (k j n) -> p k j n", k=2, j=WT)
    m.bases = part(NW)
    m.arena = sb("arena", [P, NP + P + NP + NB * (HID + 4 * D)])
    at = 0

    def take(columns, d=None, rows=P):
        nonlocal at
        at += columns
        flat = m.arena[0:rows, at - columns:at]
        return flat if d is None else flat.rearrange("p (b d) -> p b d", d=d)

    m.acc = take(NP + P)
    m.h = take(NB * D, D)
    m.xT = take(NP, rows=D)
    m.parts = m.arena[:, at - NP:at].bitcast(BF16)[:, 0:NB * 3 * D].rearrange("p (b d) -> p b d", d=3 * D)
    m.wide = m.arena[:, at:at + NB * (HID + 2 * D)]
    m.rows = take(NB * HID, HID)
    m.tmp = take(NB * D, D)
    m.cur = take(NB * D, D)
    m.x = take(NB * D, D)
    m.out = m.arena[:, NP + P:at].bitcast(F16).rearrange("p (k h n) -> p k h n", k=2, h=NB)
    m.deg = sb("deg", [P, NB])
    m.dinv1 = sb("dinv1", [P, NB])
    m.dinv3 = sb("dinv3", [P, NB])
    m.st = [sb(f"st{i}", [P, NB]) for i in range(3)]
    m.ident = sb("ident", [P, P])
    m.fast = sb("fast", [1, 1], I32)
    m.iota = sb("iota", [P, P])
    m.iota_p = sb("iota_p", [P, 1])
    m.ones = sb("ones", [1, P])
    m.w1 = sb("w1", [D, 3, D])
    m.wout = sb("wout", [D, D])
    m.b1 = sb("b1", [P, 3, D])
    m.bout = sb("bout", [P, D])
    m.wab = sb("wab", [D, 2 * HID])
    m.wc = sb("wc", [P, HID])
    m.bh = sb("bh", [P, HID])
    m.w2 = sb("w2", [HID, D])
    m.b2 = sb("b2", [P, D])
    m.wgru = sb("wgru", [P, 4 * D])
    m.bgru = sb("bgru", [P, 4 * D])
    m.w3 = sb("w3", [D, D])
    m.b3 = sb("b3", [P, D])
    m.ps = ctx.enter_context(nc.psum_tensor("ps", [P, 8, BANK], F32))

    def sem(name):
        return ctx.enter_context(nc.semaphore(name))

    m.always = edge_semaphores(sem, "", RING0)
    m.general = edge_semaphores(sem, "general_", RING)
    m.arrived = [sem(f"arrived{j}") for j in range(NPIECE)]
    m.piece_used = sem("piece_used")
    m.joined = sem("joined")
    m.dense_passes = 0
    m.block_turned, m.block_out = sem("block_turned"), sem("block_out")
    m.tabled, m.tabled_count = sem("tabled"), 0
    m.multiplied = sem("multiplied")
    m.copied = [sem("dve_copied"), sem("act_copied")]
    m.groups, m.copies = 0, [0, 0]
    return m


def load(nc, m, a):
    with nc.semaphore("loaded") as loaded, nc.semaphore("iotas") as iotas, nc.semaphore("ready") as ready, \
            nc.semaphore("based") as based, nc.semaphore("ident_zero") as ident_zero, nc.Block() as block:
        row_bias = [(m.bout, "bout"), (m.bh, "bh"), (m.b2, "b2"), (m.b3, "b3"),
                    (m.wc, "wc")]
        plain = [(m.src, "src"), (m.dst, "dst"), (m.rel, "rel"),
                 (m.w1, "w1"), (m.wout, "wout"), (m.wab, "wab"), (m.w2, "w2"), (m.w3, "w3")]
        bhh = m.cur[:, 0:3, :].rearrange("p b d -> p (b d)")
        of_gru = [(m.wgru[0:D, 0:3 * D], a["wih"]), (m.wgru[D:P, 0:2 * D], a["whh"][:, 0:2 * D]),
                  (m.wgru[D:P, 3 * D:4 * D], a["whh"][:, 2 * D:3 * D]),
                  (m.bgru[:, 0:3 * D], a["bih"].partition_broadcast(P)), (bhh, a["bhh"].partition_broadcast(P))]
        total = 16 * (len(row_bias) + len(plain) + len(of_gru) + 1)

        @block.sync
        def _(sp):
            for t, name in plain:
                sp.dma_start(t[:], a[name]).then_inc(loaded, 16)
            for t, name in row_bias:
                sp.dma_start(t[:], a[name].partition_broadcast(P)).then_inc(loaded, 16)
            for t, source in of_gru:
                sp.dma_start(t, source).then_inc(loaded, 16)
            sp.dma_start(m.b1[:], a["b1"].partition_broadcast(P)).then_inc(loaded, 16)

        @block.gpsimd
        def _(pool):
            pool.iota(m.iota[:], [[1, P]], base=0, channel_multiplier=0,
                      allow_small_or_imprecise_dtypes=True).then_inc(iotas, 1)
            pool.iota(m.iota_p[:], [[1, 1]], base=0, channel_multiplier=1,
                      allow_small_or_imprecise_dtypes=True).then_inc(iotas, 1)
            pool.memset(m.ident[:], 0.0).then_inc(ident_zero, 1)
            pool.wait_ge(ident_zero, 1)
            pool.affine_select(out=m.ident[:], in_=m.ident[:], compare_op=ALU.not_equal, fill=1.0, base=0,
                               pattern=[[-1, P]], channel_multiplier=1).then_inc(iotas, 1)

        @block.tensor
        def _(pe):
            pe.wait_ge(ready, 3)
            for c in range(4):
                w = ET // 4
                nc.tensor.matmul(m.ps[:, c, 0:w], m.ones[:], m.tmp[0:1, :, :].rearrange("p b d -> p (b d)")[:, c * w:(c + 1) * w],
                                 start=True, stop=True).then_inc(based, 1)

        @block.vector
        def _(dve):
            dve.memset(m.ones[:], 1.0).then_inc(ready, 1)
            dve.wait_ge(loaded, total)
            dve.tensor_copy(m.tmp[0:1, :, :].rearrange("p b d -> p (b d)")[:, 0:ET], m.dst[0:1, :]).then_inc(ready, 1)
            dve.memset(m.wgru[0:D, 3 * D:4 * D], 0.0)
            dve.memset(m.wgru[D:P, 2 * D:3 * D], 0.0)
            dve.tensor_tensor(m.bgru[:, 0:2 * D], m.bgru[:, 0:2 * D], bhh[:, 0:2 * D], ALU.add)
            dve.tensor_copy(m.bgru[:, 3 * D:4 * D], bhh[:, 2 * D:3 * D])
            dve.memset(m.src_rel[:, ET:], 0)
            dve.scalar_tensor_tensor(m.src_rel[:, 0:ET], m.src[:], float(R), m.rel[:], op0=ALU.mult, op1=ALU.add)
            dve.tensor_copy(m.local[:], m.dst[:]).then_inc(ready, 1)
            dve.wait_ge(ready, 3)
            dve.wait_ge(based, 4)
            w = ET // 4
            for c in range(4):
                dve.tensor_tensor(m.local[:, c * w:(c + 1) * w], m.local[:, c * w:(c + 1) * w], m.ps[:, c, 0:w],
                                  ALU.subtract)

        @block.scalar
        def _(act):
            act.wait_ge(iotas, 3)
            act.wait_ge(loaded, total)


def relation_table(nc, m, weights, xT, table):
    y = m.rows[:, 0:2 * R * D // HID, :].rearrange("p b d -> p (b d)").rearrange("p (k c) -> p k c", k=2)
    w0 = m.acc[0:D, 0:R * D]
    with nc.semaphore("w0_loaded") as w0_loaded, nc.semaphore("rel_multiplied") as multiplied, \
            nc.semaphore("rel_act_copied") as act_copied, nc.semaphore("rel_dve_copied") as dve_copied, \
            nc.semaphore("stored0") as stored0, nc.semaphore("stored1") as stored1, nc.Block() as block:
        stored = [stored0, stored1]
        t = table.rearrange("(n r) d -> n (r d)", r=R)
        half = R * D // 2

        @block.tensor
        def _(pe):
            pe.wait_ge(w0_loaded, 32)
            for b in range(NB):
                if b >= 2:
                    pe.wait_ge(act_copied, b - 1)
                    pe.wait_ge(dve_copied, b - 1)
                for q in range(4):
                    k = nc.tensor.matmul(m.ps[:, 4 * (b % 2) + q, :], m.xT[:, b * P:(b + 1) * P],
                                         w0[:, q * BANK:(q + 1) * BANK], start=True, stop=True)
                k.then_inc(multiplied, 1)

        def copy(e, b, copied, lo):
            e.wait_ge(multiplied, b + 1)
            if b >= 2:
                e.wait_ge(stored[b % 2], 16 * (b // 2))
            o = y[:, b % 2, lo * half:(lo + 1) * half]
            i = m.ps[:, 4 * (b % 2) + 2 * lo:4 * (b % 2) + 2 * lo + 2, :].rearrange("p q c -> p (q c)")
            (e.copy(o, i) if lo else e.tensor_copy(o, i)).then_inc(copied, 1)

        @block.vector
        def _(dve):
            for b in range(NB):
                copy(dve, b, dve_copied, 0)

        @block.scalar
        def _(act):
            for b in range(NB):
                copy(act, b, act_copied, 1)

        @block.sync
        def _(sp):
            sp.dma_start(w0[:], weights).then_inc(w0_loaded, 16)
            sp.dma_start(m.xT[:], xT).then_inc(w0_loaded, 16)
            for b in range(NB):
                sp.wait_ge(act_copied, b + 1)
                sp.wait_ge(dve_copied, b + 1)
                sp.dma_start(t[b * P:(b + 1) * P, :], y[:, b % 2, :]).then_inc(stored[b % 2], 16)
            for i in range(2):
                sp.wait_ge(stored[i], 16 * ((NB + 1 - i) // 2))


def window_starts(nc, m, engine, i, u):
    if u % HALF == 0:
        _, m.starts = nc.values_load_multi_w_load_instructions(
            m.dst[0:1, bass.ds(i * RING + u, HALF)], engines=(engine.engine,), min_val=0, max_val=N - 1,
            skip_runtime_bounds_check_because="a destination is one of the N nodes")
    return m.starts[u % HALF]


def edge_sum_programs(nc, m, s, rows, table, index, out):
    landed, staged, compared, summed, added, cleared = s.landed, s.staged, s.compared, s.summed, s.added, s.cleared
    tiles0, landings0, stagings0, clears0 = s.passes * ET, s.landings, s.stagings, s.clearings
    s.passes, s.landings, s.stagings, s.clearings = s.passes + 1, s.landings + ITER, s.stagings + 2 * ITER, clears0 + 1

    m.tabled_count += 1
    tabled = m.tabled_count
    blocks0 = NB * (tabled - 1)

    def sync(sp):
        sp.dma_start(table.rearrange("(b p) d -> p b d", p=P), rows).then_inc(m.tabled, 16)
        sp.wait_ge(m.tabled, 16 * tabled)

    def scalar(act):
        def stage(i, first):
            for h in range(2):
                if not first:
                    act.wait_ge(summed, tiles0 + RING * (i - 1) + HALF * (h + 1))
                act.copy(m.stage[:, h * HALF:(h + 1) * HALF],
                         index[:, bass.ds(i * RING + h * HALF, HALF)]).then_inc(staged, 1)
        stage(0, True)
        with act.Fori(1, ITER) as i:
            stage(i, False)
        for b in range(NB):
            act.wait_ge(m.block_turned, blocks0 + b + 1)
            act.copy(out[:, b, :], m.ps[:, 2 + b % 4, 0:D]).then_inc(m.block_out, 1)

    def gpsimd(pool):
        def gather(i):
            for u in range(RING):
                if u % HALF == 0:
                    pool.wait_ge(staged, stagings0 + 2 * i + u // HALF + 1)
                    pool.nop(nofuse=True)
                pool.indirect_dma_start(m.feat[:, u, 0:D], None, table,
                                        bass.IndirectOffsetOnAxis(ap=m.stage[:, u:u + 1], axis=0)
                                        ).then_inc(landed[u], 16)
        pool.wait_ge(m.tabled, 16 * tabled)
        gather(0)
        with pool.Fori(1, ITER) as i:
            gather(i)

    def tensor(pe):
        def tiles(i, first):
            for u in range(RING):
                pe.wait_ge(landed[u], 16 * landings0 + 16 * i + 16)
                pe.wait_ge(compared, tiles0 + RING * i + u + 1)
                if not (first and u < 2):
                    pe.wait_ge(added, tiles0 + RING * i + u - 1)
                nc.tensor.matmul(m.ps[0:D, u % 2, 0:P], m.feat[:, u, 0:D], m.onehot[:, u, :],
                                 start=True, stop=True).then_inc(summed, 1)
        tiles(0, True)
        with pe.Fori(1, ITER) as i:
            tiles(i, False)
        pe.wait_ge(added, tiles0 + ET)
        for b in range(NB):
            if b >= 4:
                pe.wait_ge(m.block_out, blocks0 + b - 3)
            nc.tensor.transpose(m.ps[:, 2 + b % 4, 0:D], m.acc[0:D, b * P:(b + 1) * P], m.ident[0:D, 0:D]
                                ).then_inc(m.block_turned, 1)

    def vector(dve):
        def compare(i, u):
            dve.tensor_scalar(m.onehot[:, u, :], m.iota[:], m.local[:, bass.ds(i * RING + u, 1)], None,
                              ALU.is_equal).then_inc(compared, 1)

        def add(i, u, first):
            base = window_starts(nc, m, dve, i, u)
            dve.wait_ge(summed, tiles0 + RING * i + u + 1)
            if not (first and u == 0):
                dve.wait_ge(added, tiles0 + RING * i + u)
            window = m.acc[0:D, bass.ds(base, P)]
            dve.tensor_tensor(window, window, m.ps[0:D, u % 2, 0:P], ALU.add).then_inc(added, 1)

        dve.memset(m.acc[0:D, :], 0.0).then_inc(cleared, 1)
        for u in range(RING):
            compare(0, u)
        dve.wait_ge(cleared, clears0 + 1)

        def tiles(i, first):
            for u in range(RING):
                add(i, u, first)
                compare(i + 1, u)
        tiles(0, True)
        with dve.Fori(1, ITER - 1) as i:
            tiles(i, False)
        for u in range(RING):
            add(ITER - 1, u, False)

    return {"sync": sync, "scalar": scalar, "gpsimd": gpsimd, "tensor": tensor, "vector": vector}


def windows_of_edges(nc, m, starts_dram):
    with ExitStack() as ctx:
        def sb(name, shape, dt=F32):
            return ctx.enter_context(nc.sbuf_tensor(name, shape, dt))

        def sem(name):
            return ctx.enter_context(nc.semaphore(name))

        flat = m.rows[:].rearrange("p b d -> p (b d)")
        firsts = flat[:, 0:ET]
        passed = flat[:, ET:2 * ET]
        part = flat[:, 2 * ET:3 * ET].bitcast(I32)
        cols = (NW + P - 1) // P
        edge_of = sb("edge_of", [P, 2, cols])
        before = sb("before", [P, 2, cols])
        start = sb("start", [P, cols])
        start_i = sb("start_i", [P, cols], I32)
        wide = sb("wide", [P, cols])
        wides = sb("wides", [P, 1])
        ones = sb("ones_col", [P, 1])
        iotas, step, moved, summed_wide = sem("iotas"), sem("step"), sem("moved"), sem("summed_wide")
        block = ctx.enter_context(nc.Block())

        @block.gpsimd
        def _(pool):
            pool.iota(m.key_iota[:].rearrange("p (h n) -> p h n", n=WIN), [[1, NB], [NB, WIN]], base=0,
                      channel_multiplier=0, allow_small_or_imprecise_dtypes=True)
            pool.iota(m.lo_iota[:], [[1, P]], base=0, channel_multiplier=0, allow_small_or_imprecise_dtypes=True)
            pool.iota(m.bases[:], [[-KEYS, NW]], base=0, channel_multiplier=0, allow_small_or_imprecise_dtypes=True)
            for k in range(2):
                pool.iota(edge_of[:, k, :], [[WIN, cols]], base=k * WIN, channel_multiplier=cols * WIN,
                          allow_small_or_imprecise_dtypes=True).then_inc(iotas, 1)

        @block.vector
        def _(dve):
            dve.tensor_scalar(part, m.src[:], 7, None, ALU.arith_shift_right).then_inc(step, 1)
            dve.wait_ge(step, 1)
            dve.tensor_copy(passed, part).then_inc(step, 1)
            dve.tensor_copy(m.key[:], m.dst[:]).then_inc(step, 1)
            dve.wait_ge(step, 3)
            dve.scalar_tensor_tensor(m.key[:], m.key[:], float(NB), passed, op0=ALU.mult, op1=ALU.add)
            dve.scalar_tensor_tensor(m.lo, passed, -float(P), m.src[:], op0=ALU.mult, op1=ALU.add).then_inc(step, 1)
            dve.tensor_tensor(firsts, m.dst[:], m.local[:], ALU.subtract).then_inc(step, 1)
            dve.memset(ones[:], 1.0)
            dve.wait_ge(iotas, 2)
            at = 5
            for k in range(2):
                for j in range(cols):
                    dve.wait_ge(step, at)
                    dve.tensor_scalar(passed, firsts, edge_of[:, k, j:j + 1], 0.0, ALU.is_lt, ALU.add,
                                      accum_out=before[:, k, j:j + 1]).then_inc(step, 1)
                    at += 1
            dve.wait_ge(step, at)
            dve.tensor_scalar(start[:], before[:, 0, :], -1.0, 0.0, ALU.add, ALU.max).then_inc(step, 1)
            dve.wait_ge(step, at + 1)
            dve.tensor_scalar(start[:], start[:], float(ET - WT), None, ALU.min).then_inc(step, 1)
            dve.wait_ge(step, at + 2)
            dve.tensor_copy(start_i[:], start[:]).then_inc(step, 1)
            dve.tensor_tensor(wide[:], before[:, 1, :], start[:], ALU.subtract).then_inc(step, 1)
            dve.wait_ge(step, at + 4)
            dve.tensor_scalar(wide[:], wide[:], float(WT), None, ALU.is_gt).then_inc(step, 1)
            dve.wait_ge(step, at + 5)
            dve.tensor_reduce(wides[:], wide[:], axis=AX.X, op=ALU.add).then_inc(step, 1)
            dve.wait_ge(summed_wide, 1)
            dve.tensor_scalar(m.fast[:], m.ps[0:1, 0, 0:1], 0.5, None, ALU.is_lt)

        @block.tensor
        def _(pe):
            pe.wait_ge(step, 5 + 2 * cols + 6)
            nc.tensor.matmul(m.ps[0:1, 0, 0:1], wides[:], ones[:], start=True, stop=True).then_inc(summed_wide, 1)

        @block.sync
        def _(sp):
            sp.wait_ge(step, 5 + 2 * cols + 3)
            sp.dma_start(starts_dram.rearrange("(p k) -> p k", p=P), start_i[:]).then_inc(moved, 16)
            sp.wait_ge(moved, 16)
            sp.dma_start(m.window_tile[:], starts_dram.rearrange("(a w) -> a w", a=1)).then_inc(moved, 16)
            sp.wait_ge(moved, 32)


def first_pass(nc, m, table, counts):
    s = m.always
    landed, staged, compared, summed, added, cleared = s.landed, s.staged, s.compared, s.summed, s.added, s.cleared
    feat, onehot, stage, lo_off = m.feat0, m.onehot0, m.stage0, m.lo_off
    per_chunk = CHUNK // P
    last = NB - 1
    with ExitStack() as ctx:
        def sem(name):
            return ctx.enter_context(nc.semaphore(name))

        picked, keyed, counted, kept = sem("picked"), sem("keyed"), sem("counted"), sem("kept")
        off, lo_made = sem("off"), sem("lo_made")
        stored = [sem("chunk_stored0"), sem("chunk_stored1")]
        block = ctx.enter_context(nc.Block())

        def wait(e, sem, count):
            if not isinstance(count, int) or count > 0:
                e.wait_ge(sem, count)

        def tiles_of(i):
            return LAST0 if isinstance(i, int) and i == last else RING0

        def beside(v, n):
            return range(v * n // GROUP, (v + 1) * n // GROUP)

        def load(engine, row, at, n, most):
            _, regs = nc.values_load_multi_w_load_instructions(
                row[0:1, bass.ds(at, n)], engines=(engine.engine,), min_val=0, max_val=most,
                skip_runtime_bounds_check_because="a destination is one of the N nodes; a tile is clipped")
            return regs

        @block.scalar
        def _(act):
            def restage(i, h):
                wait(act, summed, RING0 * (i - 1) + THIRD * (h + 1))
                act.copy(stage[:, h * THIRD:(h + 1) * THIRD],
                         m.src_rel[:, bass.ds(i * RING0 + h * THIRD, THIRD)]).then_inc(staged, 1)

            def choose(i, v, tile):
                act.activation(m.pick[:, v, :], m.key[:, bass.ds(tile, WT)], ACT.Identity,
                               bias=m.bases[:, bass.ds(i * GROUP + v, 1)]).then_inc(picked, 1)
                for j in range(ACT_TILES):
                    k = act.activation(lo_off[:, v % 2, j, :], m.lo_iota[:], ACT.Abs, scale=-1.0,
                                       bias=m.lo[:, bass.ds(tile + WT - ACT_TILES + j, 1)])
                k.then_inc(off, 1)
                act.wait_ge(off, i * GROUP + v + 1)
                act.activation(m.los[:, v % 2, WT - ACT_TILES:WT, :], lo_off[:, v % 2, :, :], ACT.Relu,
                               scale=-1.0, bias=1.0).then_inc(lo_made, 1)

            def keep(i, v, r, k):
                act.wait_ge(counted, i * GROUP + v + 1)
                act.copy(m.out[:, k, :, bass.ds(r * P + v * WIN, WIN)],
                         m.ps[:, 4 + v % 4, 0:KEYS].rearrange("p (h n) -> p h n", n=WIN)).then_inc(kept, 1)

            def iteration(i, r, k):
                more = not (isinstance(i, int) and i == last)
                ahead = GROUP if more else GROUP - 2
                tiles = load(act, m.window_tile, i * GROUP + 2, ahead, ET - WT)
                for v in range(GROUP):
                    keep(i, v, r, k)
                    if v < ahead:
                        choose(i + (v + 2) // GROUP, (v + 2) % GROUP, tiles[v])
                    if more and v in (5, 10, 15):
                        restage(i + 1, (v - 5) // 5)

            tiles = load(act, m.window_tile, 0, 2, ET - WT)
            for h in range(3):
                restage(0, h)
            for v in range(2):
                choose(0, v, tiles[v])
            iteration(0, 0, 0)
            with act.Fori(1, per_chunk) as r:
                iteration(r, r, 0)
            with act.Fori(0, per_chunk) as r:
                iteration(per_chunk + r, r, 1)
            with act.Fori(1, (NC - 1) // 2) as pair:
                for k in range(2):
                    act.wait_ge(stored[k], 16 * NPIECE * pair)
                    with act.Fori(0, per_chunk) as r:
                        iteration(pair * (2 * per_chunk) + k * per_chunk + r, r, k)
            act.wait_ge(stored[0], 16 * NPIECE * ((NC - 1) // 2))
            iteration(last, 0, 0)

        @block.gpsimd
        def _(pool):
            def gather(i):
                for u in range(tiles_of(i)):
                    if u % THIRD == 0:
                        pool.wait_ge(staged, 3 * i + u // THIRD + 1)
                        pool.nop(nofuse=True)
                    pool.indirect_dma_start(feat[:, u, 0:D], None, table,
                                            bass.IndirectOffsetOnAxis(ap=stage[:, u:u + 1], axis=0)
                                            ).then_inc(landed[u], 16)
            gather(0)
            with pool.Fori(1, last) as i:
                gather(i)
            gather(last)

        @block.tensor
        def _(pe):
            def count(i, v):
                w = i * GROUP + v
                pe.wait_ge(keyed, w + 1)
                pe.wait_ge(lo_made, w + 1)
                wait(pe, kept, w - 3)
                for j in range(WT):
                    k = nc.tensor.matmul(m.ps[:, 4 + v % 4, 0:KEYS], m.los[:, v % 2, j, :], m.keys[:, v % 2, j, :],
                                         start=j == 0, stop=j == WT - 1)
                k.then_inc(counted, 1)

            def total(i, u):
                g = i * RING0 + u
                pe.wait_ge(landed[u], 16 * i + 16)
                pe.wait_ge(compared, g + 1)
                wait(pe, added, g - 2)
                nc.tensor.matmul(m.ps[0:D + 1, u % 3, 0:P], feat[:, u, :], onehot[:, u % THIRD, :], start=True,
                                 stop=True).then_inc(summed, 1)

            def iteration(i):
                for v in range(GROUP):
                    count(i, v)
                    for u in beside(v, tiles_of(i)):
                        total(i, u)

            pe.wait_ge(cleared, 2)
            iteration(0)
            with pe.Fori(1, last) as i:
                iteration(i)
            iteration(last)

        @block.vector
        def _(dve):
            def keys(i, v, tile):
                w = i * GROUP + v
                wait(dve, counted, w - 1)
                for j in range(WT - ACT_TILES):
                    dve.tensor_scalar(m.los[:, v % 2, j, :], m.lo_iota[:], m.lo[:, bass.ds(tile + j, 1)], None,
                                      ALU.is_equal)
                dve.wait_ge(picked, w + 1)
                for j in range(WT):
                    k = dve.tensor_scalar(m.keys[:, v % 2, j, :], m.key_iota[:], m.pick[:, v, j:j + 1], None,
                                          ALU.is_equal)
                k.then_inc(keyed, 1)

            def compare(i, u):
                dve.tensor_scalar(onehot[:, u % THIRD, :], m.iota[:], m.local[:, bass.ds(i * RING0 + u, 1)], None,
                                  ALU.is_equal).then_inc(compared, 1)

            def add(i, u, base):
                g = i * RING0 + u
                dve.wait_ge(summed, g + 1)
                wait(dve, added, g)
                window = m.acc[0:D + 1, bass.ds(base, P)]
                dve.tensor_tensor(window, window, m.ps[0:D + 1, u % 3, 0:P], ALU.add).then_inc(added, 1)

            def iteration(i):
                more = not (isinstance(i, int) and i == last)
                ahead = GROUP if more else GROUP - 1
                tiles = load(dve, m.window_tile, i * GROUP + 1, ahead, ET - WT)
                for v in range(GROUP):
                    if v < ahead:
                        keys(i + (v + 1) // GROUP, (v + 1) % GROUP, tiles[v])
                    for u in beside(v, tiles_of(i)):
                        if u % THIRD == 0:
                            bases = load(dve, m.dst, i * RING0 + u, min(THIRD, tiles_of(i) - u), N - 1)
                        add(i, u, bases[u % THIRD])
                        if not isinstance(i, int) or i * RING0 + u + THIRD < ET:
                            compare(i, u + THIRD)

            dve.memset(m.acc[0:D + 1, :], 0.0).then_inc(cleared, 1)
            dve.memset(feat[:, :, D:D + 1], 1.0).then_inc(cleared, 1)
            for u in range(THIRD):
                compare(0, u)
            dve.wait_ge(cleared, 1)
            keys(0, 0, load(dve, m.window_tile, 0, 1, ET - WT)[0])
            iteration(0)
            with dve.Fori(1, last) as i:
                iteration(i)
            iteration(last)

        @block.sync
        def _(sp):
            for c in range(NC):
                n = CHUNK if c < NC - 1 else TAIL
                sp.wait_ge(kept, c * (CHUNK // WIN) + n // WIN)
                for j in range(NPIECE):
                    sp.dma_start(counts[c, j].rearrange("p (h n) -> p h n", n=CHUNK)[:, :, 0:n],
                                 m.out[:, c % 2, j * PIECE:(j + 1) * PIECE, 0:n]).then_inc(stored[c % 2], 16)
            for k in range(2):
                sp.wait_ge(stored[k], 16 * NPIECE * ((NC + 1 - k) // 2))
    s.passes, s.landings, s.stagings, s.clearings = 1, NB, 3 * NB, 2


def dense_sum_programs(nc, m, counts, parts, ring, out):
    passes = m.dense_passes
    m.dense_passes += 1
    chunks0, pieces0 = passes * NC, passes * NC * NPIECE
    arrived, used, joined = m.arrived, m.piece_used, m.joined
    per_chunk = CHUNK // P

    def wait(e, sem, count, so_far):
        if not isinstance(count, int) or count > 0:
            e.wait_ge(sem, so_far + count)

    def chunks(e, program):
        program(0, 0, CHUNK)
        program(1, 1, CHUNK)
        with e.Fori(1, (NC - 1) // 2) as i:
            for k in range(2):
                program(2 * i + k, k, CHUNK)
        program(NC - 1, (NC - 1) % 2, TAIL)

    def sync(sp):
        def load(c, k, n):
            for j in range(NPIECE):
                wait(sp, used, NPIECE * (c - 1) + j + 1, pieces0)
                piece = counts[bass.ds(c, 1), j].rearrange("a p (h n) -> p (a h) n", n=CHUNK)
                sp.dma_start(ring[:, j, :, 0:n], piece[:, :, 0:n]).then_inc(arrived[j], 16)
        chunks(sp, load)

    def tensor(pe):
        def multiply(c, k, n):
            wait(pe, joined, c - 1, chunks0)
            for j in range(NPIECE):
                pe.wait_ge(arrived[j], 16 * chunks0 + 16 * c + 16)
                for h in range(PIECE):
                    b = j * PIECE + h
                    for t in range(n // P):
                        last = nc.tensor.matmul(m.ps[:, per_chunk * k + t, 0:3 * D], ring[:, j, h, t * P:(t + 1) * P],
                                                parts[:, b, :], start=b == 0, stop=b == NB - 1)
                last.then_inc(used, 1)
        chunks(pe, multiply)

    def vector(dve):
        def join(c, k, n):
            dve.wait_ge(used, pieces0 + NPIECE * (c + 1))
            sums = m.ps[:, per_chunk * k:per_chunk * k + n // P, 0:3 * D].rearrange("p t (q d) -> p t d q", q=3)
            dve.tensor_reduce(out[:, bass.ds(c * per_chunk, n // P), :], sums, axis=AX.X, op=ALU.add
                              ).then_inc(joined, 1)
        chunks(dve, join)

    return {"sync": sync, "tensor": tensor, "vector": vector}


def scale_and_split(nc, m, rows, scale, parts):
    rest = m.tmp[:]
    halves = (slice(0, NB // 2), slice(NB // 2, NB))
    with nc.semaphore("rounded") as rounded, nc.semaphore("left") as left, nc.Block() as block:
        @block.vector
        def _(dve):
            for h in halves:
                n = h.stop - h.start
                dve.tensor_tensor(rows[:, h, :], rows[:, h, :], scale[:, h].unsqueeze(2).broadcast_to([P, n, D]),
                                  ALU.mult).then_inc(left, 1)
            for k in range(2):
                for i, h in enumerate(halves):
                    dve.wait_ge(rounded, 2 * k + i + 1)
                    of = rows if k == 0 else rest
                    dve.tensor_tensor(rest[:, h, :], of[:, h, :], parts[:, h, k * D:(k + 1) * D],
                                      ALU.subtract).then_inc(left, 1)

        @block.scalar
        def _(act):
            for k in range(3):
                for i, h in enumerate(halves):
                    act.wait_ge(left, 2 * k + i + 1)
                    of = rows if k == 0 else rest
                    act.copy(parts[:, h, k * D:(k + 1) * D], of[:, h, :]).then_inc(rounded, 1)


def neighbour_sum(nc, m, rows, scale, table, counts):
    with ExitStack() as ctx:
        parts = m.parts
        scale_and_split(nc, m, rows, scale, parts)
        ring = m.wide.bitcast(F16).rearrange("p (j h n) -> p j h n", j=NPIECE, h=PIECE)
        dense = dense_sum_programs(nc, m, counts, parts, ring, m.sum_rows)
        gather = edge_sum_programs(nc, m, m.general, rows, table, m.src, m.sum_rows)
        block = ctx.enter_context(nc.Block())

        def either(engine, name):
            fast = nc.values_load(m.fast[:], engines=(engine.engine,), min_val=0, max_val=1,
                                  skip_runtime_bounds_check_because="the result of a comparison")
            with engine.If(fast == 1):
                if name in dense:
                    dense[name](engine)
                else:
                    engine.nop()
            with engine.Else():
                if name in gather:
                    gather[name](engine)
                else:
                    engine.nop()

        @block.sync
        def _(sp):
            either(sp, "sync")

        @block.gpsimd
        def _(pool):
            either(pool, "gpsimd")

        @block.tensor
        def _(pe):
            either(pe, "tensor")

        @block.scalar
        def _(act):
            either(act, "scalar")

        @block.vector
        def _(dve):
            either(dve, "vector")


def edge_mlp_sum(nc, m, table, q):
    with ExitStack() as ctx:
        sem = lambda name: ctx.enter_context(nc.semaphore(name))
        s = m.always
        landed, staged, compared, summed, added, cleared = s.landed, s.staged, s.compared, s.summed, s.added, s.cleared
        tiles0, landings0, stagings0, clears0 = s.passes * ET, s.landings, s.stagings, s.clearings
        fetched = [sem(f"fetched{u}") for u in range(HALF)]
        names = ("spread", "turned", "hidden", "biased", "activated")
        spread, turned, hidden, biased, activated = map(sem, names)
        flat = m.h[:].rearrange("p b d -> p (b d)").rearrange("p (k c) -> p k c", c=HID) if NB % 2 == 0 else \
            m.h[:, 0:NB - 1, :].rearrange("p (k two) d -> p k (two d)", two=2)
        other = m.tmp[:, 0:NB - 1, :].rearrange("p (k two) d -> p k (two d)", two=2)
        window_q = flat[:, 0:HALF, :]
        turned_hot = other[:, 0:2, :]
        act_in = other[:, 2:4, :]
        act_out = other[:, 4:6, :]
        block = ctx.enter_context(nc.Block())

        def wait(e, sem, count, so_far=0):
            if not isinstance(count, int) or count > 0:
                e.wait_ge(sem, so_far + count)


        @block.scalar
        def _(act):
            def stage(i, h):
                act.copy(m.stage[:, h * HALF:(h + 1) * HALF],
                         m.src[:, bass.ds(i * RING + h * HALF, HALF)]).then_inc(staged, 1)

            def turn(i, u):
                g = i * RING + u
                act.wait_ge(spread, g + 1)
                wait(act, hidden, g - 1)
                act.copy(turned_hot[:, u % 2, :], m.ps[:, 2 + u % 2, 0:P]).then_inc(turned, 1)

            def relu(i, u):
                g = i * RING + u
                act.wait_ge(hidden, g + 1)
                wait(act, summed, g - 1, tiles0)
                act.activation(act_out[:, u % 2, :], m.ps[:, 4 + u % 2, 0:HID], ACT.Relu).then_inc(activated, 1)

            def steps(i, last):
                for u in range(RING):
                    if not last or u + 2 < RING:
                        turn(i, u + 2)
                    if not last or u + 1 < RING:
                        relu(i, u + 1)
                    if (u + 1) % HALF == HALF - 1 and not last:
                        stage(i + 1, u // HALF)

            for h in range(2):
                stage(0, h)
            turn(0, 0)
            turn(0, 1)
            relu(0, 0)
            steps(0, False)
            with act.Fori(1, ITER - 1) as i:
                steps(i, False)
            steps(ITER - 1, True)

        @block.gpsimd
        def _(pool):
            def gather(i):
                for u in range(RING):
                    if u % HALF == 0:
                        pool.wait_ge(staged, stagings0 + 2 * i + u // HALF + 1)
                        pool.nop(nofuse=True)
                    pool.indirect_dma_start(m.feat[:, u, :], None, table,
                                            bass.IndirectOffsetOnAxis(ap=m.stage[:, u:u + 1], axis=0)
                                            ).then_inc(landed[u], 16)
            gather(0)
            with pool.Fori(1, ITER) as i:
                gather(i)

        @block.sync
        def _(sp):
            def fetch(i):
                for u in range(RING):
                    g = i * RING + u
                    base = window_starts(nc, m, sp, i, u)
                    wait(sp, hidden, g + 1 - HALF)
                    sp.dma_start(window_q[:, u % HALF, :], q[bass.ds(base, P), :]).then_inc(fetched[u % HALF], 16)
            fetch(0)
            with sp.Fori(1, ITER) as i:
                fetch(i)

        @block.tensor
        def _(pe):
            def turn(i, u):
                g = i * RING + u
                pe.wait_ge(compared, tiles0 + g + 1)
                wait(pe, turned, g - 1)
                nc.tensor.transpose(m.ps[:, 2 + u % 2, 0:P], m.onehot[:, u % RING, :], m.ident[:]).then_inc(spread, 1)

            def hide(i, u):
                g = i * RING + u
                wait(pe, activated, g - 1)
                pe.wait_ge(biased, g + 1)
                nc.tensor.matmul(m.ps[:, 4 + u % 2, 0:HID], m.ident[:], act_in[:, u % 2, :], start=True, stop=False)
                pe.wait_ge(turned, g + 1)
                pe.wait_ge(fetched[u % HALF], 32 * i + 16 * (u // HALF) + 16)
                nc.tensor.matmul(m.ps[:, 4 + u % 2, 0:HID], turned_hot[:, u % 2, :], window_q[:, u % HALF, :],
                                 start=False, stop=True).then_inc(hidden, 1)

            def total(i, u):
                g = i * RING + u
                wait(pe, added, g - 1, tiles0)
                pe.wait_ge(activated, g + 1)
                nc.tensor.matmul(m.ps[:, u % 2, 0:P], act_out[:, u % 2, :], m.onehot[:, u, :], start=True,
                                 stop=True).then_inc(summed, 1)

            def steps(i, last):
                for u in range(RING):
                    if not last or u + 2 < RING:
                        turn(i, u + 2)
                    if not last or u + 1 < RING:
                        hide(i, u + 1)
                    total(i, u)

            turn(0, 0)
            turn(0, 1)
            hide(0, 0)
            steps(0, False)
            with pe.Fori(1, ITER - 1) as i:
                steps(i, False)
            steps(ITER - 1, True)

        @block.vector
        def _(dve):
            def compare(i, u):
                dve.tensor_scalar(m.onehot[:, u, :], m.iota[:], m.local[:, bass.ds(i * RING + u, 1)], None,
                                  ALU.is_equal).then_inc(compared, 1)

            def bias(i, u):
                g = i * RING + u
                dve.wait_ge(landed[u % RING], 16 * landings0 + 16 * i + 16 * (u // RING) + 16)
                wait(dve, hidden, g - 1)
                dve.scalar_tensor_tensor(act_in[:, u % 2, :], m.wc[:], m.attr[:, bass.ds(g, 1)],
                                         m.feat[:, u % RING, :], op0=ALU.mult, op1=ALU.add).then_inc(biased, 1)

            def add(i, u):
                g = i * RING + u
                base = window_starts(nc, m, dve, i, u)
                dve.wait_ge(summed, tiles0 + g + 1)
                wait(dve, added, g, tiles0)
                window = m.acc[:, bass.ds(base, P)]
                dve.tensor_tensor(window, window, m.ps[:, u % 2, 0:P], ALU.add).then_inc(added, 1)

            def steps(i, last):
                for u in range(RING):
                    if not last or u + 2 < RING:
                        bias(i, u + 2)
                    add(i, u)
                    if not last:
                        compare(i + 1, u)

            dve.memset(m.acc[:], 0.0).then_inc(cleared, 1)
            for u in range(RING):
                compare(0, u)
            bias(0, 0)
            bias(0, 1)
            dve.wait_ge(cleared, clears0 + 1)
            steps(0, False)
            with dve.Fori(1, ITER - 1) as i:
                steps(i, False)
            steps(ITER - 1, True)


def products(nc, m, name, width, per_bank, operands, dest):
    groups = [range(g, min(g + per_bank, NB)) for g in range(0, NB, per_bank)]
    multiplied, copied = m.multiplied, m.copied
    groups0, copies0 = m.groups, list(m.copies)
    m.groups += len(groups)
    m.copies = [copies0[k] + (len(groups) + 1 - k) // 2 for k in range(2)]
    with nc.Block() as block:
        @block.tensor
        def _(pe):
            for g, blocks in enumerate(groups):
                if g >= 8:
                    pe.wait_ge(copied[g % 2], copies0[g % 2] + (g - 8) // 2 + 1)
                for j, b in enumerate(blocks):
                    pairs = operands(b)
                    for k, (w, x) in enumerate(pairs):
                        last = nc.tensor.matmul(m.ps[0:w.shape[1], g % 8, j * width:(j + 1) * width], w, x,
                                                start=k == 0, stop=k == len(pairs) - 1)
                last.then_inc(multiplied, 1)

        def copy(e, g, put):
            blocks = groups[g]
            e.wait_ge(multiplied, groups0 + g + 1)
            rows = operands(0)[0][0].shape[1]
            put(dest(blocks[0], len(blocks)), m.ps[0:rows, g % 8, 0:len(blocks) * width]).then_inc(copied[g % 2], 1)

        @block.vector
        def _(dve):
            for g in range(0, len(groups), 2):
                copy(dve, g, dve.tensor_copy)

        @block.scalar
        def _(act):
            for g in range(1, len(groups), 2):
                copy(act, g, act.copy)


def transpose_rows(nc, m, rows):
    products(nc, m, "turn", P, 4, lambda b: [(rows[:, b, :], m.ident[:])],
             lambda b, n: m.xT[:, b * P:(b + n) * P])


def project(nc, m, w, out, width):
    per = BANK // width
    products(nc, m, "project", width, per, lambda b: [(m.xT[:, b * P:(b + 1) * P], w)],
             lambda b, n: out[:, b:b + n, :].rearrange("p b d -> p (b d)"))


def sums_to_rows(nc, m, k, w, out, width):
    products(nc, m, "sums", width, BANK // width, lambda b: [(m.acc[0:k, b * P:(b + 1) * P], w)],
             lambda b, n: out[:, b:b + n, 0:width])


def per_node(t):
    return t[:, :].unsqueeze(2).broadcast_to([P, NB, D])


def per_feature(t, width=D):
    return t.unsqueeze(1).broadcast_to([P, NB, width])


def layer_norm(nc, m, update, out_dram=None):
    total, mean, rstd = m.st
    with nc.semaphore("step") as step, nc.semaphore("stored") as stored, nc.Block() as block:
        @block.vector
        def _(dve):
            dve.tensor_tensor(m.x[:], m.x[:], update, ALU.add).then_inc(step, 1)
            dve.wait_ge(step, 1)
            dve.tensor_reduce(total[:], m.x[:], axis=AX.X, op=ALU.add).then_inc(step, 1)
            dve.wait_ge(step, 2)
            dve.tensor_scalar(mean[:], total[:], 1.0 / D, None, ALU.mult).then_inc(step, 1)
            dve.wait_ge(step, 3)
            dve.tensor_tensor(m.x[:], m.x[:], per_node(mean), ALU.subtract).then_inc(step, 1)
            dve.wait_ge(step, 5)
            dve.tensor_reduce(total[:], m.tmp[:], axis=AX.X, op=ALU.add).then_inc(step, 1)
            dve.wait_ge(step, 6)
            dve.tensor_scalar(total[:], total[:], 1.0 / D, EPS, ALU.mult, ALU.add).then_inc(step, 1)
            dve.wait_ge(step, 8)
            dve.reciprocal(rstd[:], mean[:]).then_inc(step, 1)
            dve.wait_ge(step, 9)
            dve.tensor_tensor(m.x[:], m.x[:], per_node(rstd), ALU.mult).then_inc(step, 1)

        @block.scalar
        def _(act):
            act.wait_ge(step, 4)
            act.activation(m.tmp[:], m.x[:], ACT.Square).then_inc(step, 1)
            act.wait_ge(step, 7)
            act.activation(mean[:], total[:], ACT.Sqrt).then_inc(step, 1)

        if out_dram is not None:
            @block.sync
            def _(sp):
                sp.wait_ge(step, 10)
                full = N // P
                sp.dma_start(out_dram[0:full * P, :].rearrange("(b p) d -> p b d", p=P),
                             m.x[:, 0:full, :]).then_inc(stored, 16)
                sp.dma_start(out_dram[full * P:N, :], m.x[0:N - full * P, full, :]).then_inc(stored, 16)
                sp.wait_ge(stored, 32)


def degrees(nc, m):
    with nc.semaphore("step") as step, nc.Block() as block:
        @block.vector
        def _(dve):
            dve.tensor_copy(m.deg[:], m.rows[:, :, D]).then_inc(step, 1)
            dve.wait_ge(step, 1)
            dve.tensor_scalar(m.st[0][:], m.deg[:], 1.0, None, ALU.add).then_inc(step, 1)
            dve.tensor_scalar(m.st[1][:], m.deg[:], 1.0, None, ALU.max).then_inc(step, 1)
            dve.wait_ge(step, 5)
            dve.reciprocal(m.dinv1[:], m.st[2][:]).then_inc(step, 1)
            dve.reciprocal(m.st[0][:], m.dinv3[:]).then_inc(step, 1)
            dve.wait_ge(step, 7)
            dve.scalar_tensor_tensor(m.dinv3[:], m.deg[:], 0.0, m.st[0][:], op0=ALU.is_gt, op1=ALU.mult)

        @block.scalar
        def _(act):
            act.wait_ge(step, 3)
            act.activation(m.st[2][:], m.st[0][:], ACT.Sqrt).then_inc(step, 1)
            act.activation(m.dinv3[:], m.st[1][:], ACT.Sqrt).then_inc(step, 1)


def source_and_target_tables(nc, m, p_table, q_table):
    both = m.wide.rearrange("p (b d) -> p b d", b=NB)
    p, q = both[:, :, 0:HID], both[:, :, HID:2 * HID]
    products(nc, m, "project", 2 * HID, 2, lambda b: [(m.xT[:, b * P:(b + 1) * P], m.wab[:])],
             lambda b, n: both[:, b:b + n, :].rearrange("p b d -> p (b d)"))
    with nc.semaphore("biased") as biased, nc.semaphore("stored") as stored, nc.Block() as block:
        @block.vector
        def _(dve):
            dve.tensor_tensor(q, q, per_feature(m.bh[:], HID), ALU.add).then_inc(biased, 1)

        @block.sync
        def _(sp):
            sp.dma_start(p_table.rearrange("(b p) d -> p b d", p=P), p).then_inc(stored, 16)
            sp.dma_start(q_table[NP:NP + P, :], m.ident[:]).then_inc(stored, 16)
            sp.wait_ge(biased, 1)
            sp.dma_start(q_table[0:NP, :].rearrange("(b p) d -> p b d", p=P), q).then_inc(stored, 16)
            sp.wait_ge(stored, 48)


def gcn_finish(nc, m, bias):
    r = m.sum_rows
    with nc.semaphore("step") as step, nc.Block() as block:
        @block.vector
        def _(dve):
            dve.tensor_tensor(m.cur[:], r, m.h[:], ALU.add).then_inc(step, 1)
            dve.wait_ge(step, 1)
            dve.tensor_tensor(m.cur[:], m.cur[:], per_node(m.dinv1), ALU.mult).then_inc(step, 1)
            dve.wait_ge(step, 2)
            dve.tensor_tensor(m.cur[:], m.cur[:], per_feature(bias), ALU.add).then_inc(step, 1)
            dve.wait_ge(step, 3)
            dve.tensor_scalar(m.cur[:], m.cur[:], 0.0, None, ALU.max)


def add_bias(nc, m, rows, bias, scale=None, by_degree=False, beside=None):
    with nc.semaphore("step") as step, nc.Block() as block:
        if beside is not None:
            @block.scalar
            def _(act):
                act.copy(beside, m.x[:])

        @block.vector
        def _(dve):
            if scale is not None:
                dve.tensor_tensor(rows, rows, per_node(scale), ALU.mult).then_inc(step, 1)
                dve.wait_ge(step, 1)
            if by_degree:
                dve.tensor_tensor(m.tmp[:], per_feature(bias), per_node(m.deg), ALU.mult).then_inc(step, 1)
                dve.wait_ge(step, 1)
                dve.tensor_tensor(rows, rows, m.tmp[:], ALU.add)
            else:
                dve.tensor_tensor(rows, rows, per_feature(bias), ALU.add)


def gru(nc, m):
    products(nc, m, "turn", P, 4, lambda b: [(m.rows[:, b, :], m.ident[:])], lambda b, n: m.acc[:, b * P:(b + n) * P])
    gates = m.wide.rearrange("p (b g) -> p b g", b=NB)
    products(nc, m, "gates", 4 * D, 2, lambda b: [(m.acc[:, b * P:(b + 1) * P], m.wgru[:])],
             lambda b, n: gates[:, b:b + n, :].rearrange("p b g -> p (b g)"))
    r, z, i_n, h_n = (gates[:, :, k * D:(k + 1) * D] for k in range(4))
    t = m.h[:]
    with nc.semaphore("step") as step, nc.Block() as block:
        @block.vector
        def _(dve):
            dve.tensor_tensor(r, r, per_feature(m.bgru[:, 0:D]), ALU.add).then_inc(step, 1)
            dve.tensor_tensor(h_n, h_n, per_feature(m.bgru[:, 3 * D:4 * D]), ALU.add)
            dve.tensor_tensor(z, z, per_feature(m.bgru[:, D:2 * D]), ALU.add)
            dve.tensor_tensor(i_n, i_n, per_feature(m.bgru[:, 2 * D:3 * D]), ALU.add).then_inc(step, 1)
            dve.wait_ge(step, 3)
            dve.tensor_tensor(t, h_n, r, ALU.mult).then_inc(step, 1)
            dve.wait_ge(step, 4)
            dve.tensor_tensor(t, t, i_n, ALU.add).then_inc(step, 1)
            dve.wait_ge(step, 7)
            dve.tensor_tensor(r, m.x[:], t, ALU.subtract).then_inc(step, 1)
            dve.wait_ge(step, 8)
            dve.tensor_tensor(r, r, z, ALU.mult).then_inc(step, 1)
            dve.wait_ge(step, 9)
            dve.tensor_tensor(t, r, t, ALU.add)

        @block.scalar
        def _(act):
            act.wait_ge(step, 1)
            act.activation(r, r, ACT.Sigmoid).then_inc(step, 1)
            act.wait_ge(step, 5)
            act.activation(t, t, ACT.Tanh).then_inc(step, 1)
            act.activation(z, z, ACT.Sigmoid).then_inc(step, 1)


def build(nc, a, out):
    rel_table = nc.dram_tensor("rel_table", (NP * R, D), F32).ap()
    h_table = nc.dram_tensor("h_table", (NP, D), F32).ap()
    p_table = nc.dram_tensor("p_table", (NP, HID), F32).ap()
    counts = nc.dram_tensor("counts", (NC, NPIECE, P, PIECE * CHUNK), F16).ap()
    starts = nc.dram_tensor("window_starts", ((NW + P - 1) // P * P,), I32).ap()
    q_table = nc.dram_tensor("q_table", (NP + P, HID), F32).ap()
    with ExitStack() as ctx:
        m = alloc(nc, ctx)
        load(nc, m, a)
        windows_of_edges(nc, m, starts)
        relation_table(nc, m, a["w0"], a["xT"], rel_table)
        first_pass(nc, m, rel_table, counts)
        with nc.semaphore("late_loaded") as late_loaded:
            with nc.Block() as block:
                @block.sync
                def _(sp):
                    sp.dma_start(m.x[:], a["x"].rearrange("(b p) d -> p b d", p=P)).then_inc(late_loaded, 16)
                    sp.dma_start(m.attr[:], a["attr"]).then_inc(late_loaded, 16)
            sums_to_rows(nc, m, D + 1, m.ident[0:D + 1, 0:D + 1], m.rows, D + 1)
            degrees(nc, m)
            with nc.Block() as block:
                @block.sync
                def _(sp):
                    sp.wait_ge(late_loaded, 32)
        layer_norm(nc, m, m.rows[:, :, 0:D])
        for i in range(3):
            transpose_rows(nc, m, m.cur if i else m.x)
            project(nc, m, m.w1[:, i, :], m.h, D)
            neighbour_sum(nc, m, m.h[:], m.dinv1, h_table, counts)
            gcn_finish(nc, m, m.b1[:, i, :])
        transpose_rows(nc, m, m.cur)
        project(nc, m, m.wout[:], m.h, D)
        add_bias(nc, m, m.h[:], m.bout[:])
        layer_norm(nc, m, m.h[:])
        transpose_rows(nc, m, m.x)
        source_and_target_tables(nc, m, p_table, q_table)
        edge_mlp_sum(nc, m, p_table, q_table)
        sums_to_rows(nc, m, HID, m.w2[:], m.rows, D)
        add_bias(nc, m, m.rows[:, :, 0:D], m.b2[:], by_degree=True, beside=m.rows[:, :, D:2 * D])
        gru(nc, m)
        layer_norm(nc, m, m.h[:])
        transpose_rows(nc, m, m.x)
        project(nc, m, m.w3[:], m.h, D)
        neighbour_sum(nc, m, m.h[:], m.dinv3, h_table, counts)
        add_bias(nc, m, m.sum_rows, m.b3[:], scale=m.dinv3)
        layer_norm(nc, m, m.sum_rows, out)


def kernel(**inputs):
    import numpy as _np
    import concourse.bacc as _bacc
    from concourse import mybir as _mybir
    from concourse.bass_utils import run_bass_kernel_spmd as _run

    v = {k: _np.asarray(x) for k, x in inputs.items()}

    def by_tile(x):
        out = _np.zeros((ET * P,), x.dtype)
        out[:E] = x.reshape(-1)
        return _np.ascontiguousarray(out.reshape(ET, P).T)

    x = _np.zeros((NP, D), v["x"].dtype)
    x[:N] = v["x"]
    w1 = v["L2_gnn_W1"]
    laid = {
        "x": x, "xT": x.T, "src": by_tile(v["src"]), "dst": by_tile(v["dst"]), "rel": by_tile(v["edge_type_32"]),
        "attr": by_tile(v["edge_weight1"]), "w0": v["L0_gnn_weight"].transpose(1, 0, 2).reshape(D, R * D),
        "w1": v["L1_gnn_Ws"].transpose(1, 0, 2), "b1": v["L1_gnn_bs"], "wout": v["L1_gnn_W_out"],
        "bout": v["L1_gnn_b_out"], "wab": _np.concatenate([w1[:, :D].T, w1[:, D:2 * D].T], axis=1), "wc": w1[:, 2 * D],
        "bh": v["L2_gnn_b1"], "w2": v["L2_gnn_W2"].T, "b2": v["L2_gnn_b2"], "wih": v["L2_gnn_W_ih"].T,
        "whh": v["L2_gnn_W_hh"].T, "bih": v["L2_gnn_b_ih"], "bhh": v["L2_gnn_b_hh"], "w3": v["L3_gnn_weight"],
        "b3": v["L3_gnn_bias"],
    }
    nc = _bacc.Bacc("TRN2", target_bir_lowering=False, num_devices=1)
    arrays, a = {}, {}
    for name, x in laid.items():
        x = _np.ascontiguousarray(x)
        arrays[f"in_{name}"] = x
        a[name] = nc.dram_tensor(f"in_{name}", x.shape, _mybir.dt.from_np(x.dtype), kind="ExternalInput").ap()
    out = nc.dram_tensor("out_x", (N, D), _mybir.dt.float32, kind="ExternalOutput").ap()
    build(nc, a, out)
    r = _run(nc, [arrays], core_ids=[0])
    return r.results[0]["out_x"]
```
